# Optimizing a Trainium2 kernel written in Bass

```python
import numpy as np
import jax
import jax.numpy as jnp

def _softmax(x, axis=-1):
    return jax.nn.softmax(x, axis=axis)

def _gelu(x):
    return jax.nn.gelu(x, approximate=True)

def _silu(x):
    return jax.nn.silu(x)

def _sigmoid(x):
    return jax.nn.sigmoid(x)

def _layernorm(x, axis=-1, eps=1e-05):
    m = jnp.mean(x, axis=axis, keepdims=True)
    v = jnp.var(x, axis=axis, keepdims=True)
    return (x - m) / jnp.sqrt(v + eps)

def _scatter_add(tgt, idx, src, axis=0):
    return tgt.at[idx].add(src)

def _segment_sum(src, seg, n):
    return jax.ops.segment_sum(src, seg, n)
kernel_name = 'mk_decoder_postln_d1_seqx_r4_7e9924'

def setup_inputs(seed: int=0):
    np.random.seed(seed)
    _w = jnp.asarray

    def _rec_inputs():
        import jax
        import jax.numpy as jnp
        _rk = jax.random.key(seed)
        x = 7.22e-05 + 1 * jax.random.normal(jax.random.fold_in(_rk, 1), (4, 1024, 256), jnp.float32)
        _lenS = 1024 - jax.random.randint(jax.random.fold_in(_rk, 7), (4,), 0, max(1, 1024 // 4) + 1, jnp.int32)
        _lenS2 = 77 - jax.random.randint(jax.random.fold_in(_rk, 8), (4,), 0, max(1, 77 // 4) + 1, jnp.int32)
        _ctx_1024P = jax.random.normal(jax.random.fold_in(_rk, 11), (4, 16, 256), jnp.float32)
        _ctx_1024c = jax.random.dirichlet(jax.random.fold_in(_rk, 511), 0.3 * jnp.ones((16,), jnp.float32), (4, 77))
        _ctx_1024t = jnp.einsum('bsk,bkd->bsd', _ctx_1024c, _ctx_1024P)
        _ctx_1024t = _ctx_1024t * jax.lax.rsqrt(jnp.mean(jnp.square(_ctx_1024t)) + 1e-12) * 0.953939
        ctx_1024 = 4.13588e-05 + 0.999923 * (_ctx_1024t + 0.3 * jax.random.normal(jax.random.fold_in(_rk, 611), (4, 77, 256), jnp.float32))
        return (x, ctx_1024)
    x, ctx_1024 = _rec_inputs()

    def _L0_attn_setup():
        import jax, jax.numpy as jnp
        import numpy as np
        D_MODEL = 256
        NUM_HEADS = 16
        HEAD_DIM = D_MODEL // NUM_HEADS
        key = jax.random.key(seed)
        ks = jax.random.split(key, 5)
        B, S = (1, 1024)
        scale = 0.02
        return {'x': jax.random.normal(ks[0], (B, S, D_MODEL), dtype=jnp.float32), 'w_q': jax.random.normal(ks[1], (D_MODEL, D_MODEL), dtype=jnp.float32) * scale, 'w_k': jax.random.normal(ks[2], (D_MODEL, D_MODEL), dtype=jnp.float32) * scale, 'w_v': jax.random.normal(ks[3], (D_MODEL, D_MODEL), dtype=jnp.float32) * scale, 'w_o': jax.random.normal(ks[4], (D_MODEL, D_MODEL), dtype=jnp.float32) * scale}
    _L0_attn_all = _L0_attn_setup()
    _L0_attn_in = {k: v for k, v in _L0_attn_all.items() if k in ('w_q', 'w_k', 'w_v', 'w_o')}
    del _L0_attn_all

    def _L0_xattn_setup():
        import jax, jax.numpy as jnp
        import numpy as np
        B, S, D = (4, 512, 256)
        KEY_DIM, VALUE_DIM = (256, 256)
        BETA = 1.0 / np.sqrt(D)
        key = jax.random.key(seed)
        ks = jax.random.split(key, 9)
        inv = 1.0 / np.sqrt(D)
        return {'query': jax.random.normal(ks[0], (B, S, D), dtype=jnp.float32), 'key': jax.random.normal(ks[1], (B, S, D), dtype=jnp.float32), 'value': jax.random.normal(ks[2], (B, S, D), dtype=jnp.float32), 'Wq': jax.random.normal(ks[3], (D, KEY_DIM), dtype=jnp.float32) * inv, 'bq': jnp.zeros((KEY_DIM,), dtype=jnp.float32), 'Wk': jax.random.normal(ks[4], (D, KEY_DIM), dtype=jnp.float32) * inv, 'bk': jnp.zeros((KEY_DIM,), dtype=jnp.float32), 'Wv': jax.random.normal(ks[5], (D, VALUE_DIM), dtype=jnp.float32) * inv, 'bv': jnp.zeros((VALUE_DIM,), dtype=jnp.float32)}
    _L0_xattn_all = _L0_xattn_setup()
    _L0_xattn_in = {k: v for k, v in _L0_xattn_all.items() if k in ('Wq', 'bq', 'Wk', 'bk', 'Wv', 'bv')}
    del _L0_xattn_all

    def _L0_ffn_setup():
        import jax, jax.numpy as jnp
        import numpy as np
        B, S, H, F, E, K = (4, 512, 256, 1024, 8, 2)
        key = jax.random.key(seed)
        ks = jax.random.split(key, 4)
        sc = lambda d: 1.0 / np.sqrt(d)
        return {'x': jax.random.normal(ks[0], (B, S, H), jnp.float32), 'gate_w': jax.random.normal(ks[1], (H, E), jnp.float32) * sc(H), 'gate_b': jnp.zeros((E,), jnp.float32), 'w1': jax.random.normal(ks[2], (E, H, F), jnp.float32) * sc(H), 'b1': jnp.zeros((E, F), jnp.float32), 'w2': jax.random.normal(ks[3], (E, F, H), jnp.float32) * sc(F), 'b2': jnp.zeros((E, H), jnp.float32)}
    _L0_ffn_all = _L0_ffn_setup()
    _L0_ffn_in = {k: v for k, v in _L0_ffn_all.items() if k in ('gate_w', 'gate_b', 'w1', 'b1', 'w2', 'b2')}
    del _L0_ffn_all
    return {'x': x, 'ctx_1024': ctx_1024, 'L0_attn_w_q': _L0_attn_in['w_q'], 'L0_attn_w_k': _L0_attn_in['w_k'], 'L0_attn_w_v': _L0_attn_in['w_v'], 'L0_attn_w_o': _L0_attn_in['w_o'], 'L0_xattn_Wq': _L0_xattn_in['Wq'], 'L0_xattn_bq': _L0_xattn_in['bq'], 'L0_xattn_Wk': _L0_xattn_in['Wk'], 'L0_xattn_bk': _L0_xattn_in['bk'], 'L0_xattn_Wv': _L0_xattn_in['Wv'], 'L0_xattn_bv': _L0_xattn_in['bv'], 'L0_ffn_gate_w': _L0_ffn_in['gate_w'], 'L0_ffn_gate_b': _L0_ffn_in['gate_b'], 'L0_ffn_w1': _L0_ffn_in['w1'], 'L0_ffn_b1': _L0_ffn_in['b1'], 'L0_ffn_w2': _L0_ffn_in['w2'], 'L0_ffn_b2': _L0_ffn_in['b2']}

def reference(x, ctx_1024, L0_attn_w_q, L0_attn_w_k, L0_attn_w_v, L0_attn_w_o, L0_xattn_Wq, L0_xattn_bq, L0_xattn_Wk, L0_xattn_bk, L0_xattn_Wv, L0_xattn_bv, L0_ffn_gate_w, L0_ffn_gate_b, L0_ffn_w1, L0_ffn_b1, L0_ffn_w2, L0_ffn_b2):
    import jax
    import jax.numpy as jnp

    def _L0_attn_ref(x, w_q, w_k, w_v, w_o):
        import jax, jax.numpy as jnp
        import numpy as np
        D_MODEL = 256
        NUM_HEADS = 16
        HEAD_DIM = D_MODEL // NUM_HEADS
        B, S, _ = x.shape
        q = x @ w_q.T
        k = x @ w_k.T
        v = x @ w_v.T
        q = q.reshape(B, S, NUM_HEADS, HEAD_DIM)
        k = k.reshape(B, S, NUM_HEADS, HEAD_DIM)
        v = v.reshape(B, S, NUM_HEADS, HEAD_DIM)
        scale = HEAD_DIM ** (-0.5)
        scores = jnp.einsum('bqhd,bkhd->bhqk', q, k) * scale
        weights = jax.nn.softmax(scores, axis=-1)
        out = jnp.einsum('bhqk,bkhd->bqhd', weights, v)
        concat = out.reshape(B, S, D_MODEL)
        return concat @ w_o.T

    def _L0_xattn_ref(query, key, value, Wq, bq, Wk, bk, Wv, bv):
        import jax, jax.numpy as jnp
        import numpy as np
        B, S, D = (4, 512, 256)
        KEY_DIM, VALUE_DIM = (256, 256)
        BETA = 1.0 / np.sqrt(D)
        q = query @ Wq + bq
        k = key @ Wk + bk
        v = value @ Wv + bv
        scores = jnp.einsum('bik,bjk->bij', q, k)
        A = jax.nn.softmax(BETA * scores, axis=-1)
        return jnp.einsum('bij,bjk->bik', A, v)

    def _L0_ffn_ref(x, gate_w, gate_b, w1, b1, w2, b2):
        import jax, jax.numpy as jnp
        import numpy as np
        B, S, H, F, E, K = (4, 512, 256, 1024, 8, 2)
        Bb, Ss, Hh = x.shape
        xf = x.reshape(-1, Hh)
        gate = jax.nn.softmax(xf @ gate_w + gate_b)
        topv, topi = jax.lax.top_k(gate, K)
        topv = topv / topv.sum(-1, keepdims=True)
        combine = (jax.nn.one_hot(topi, gate.shape[-1], dtype=xf.dtype) * topv[..., None]).sum(1)

        def body(acc, p):
            w1e, b1e, w2e, b2e, ce = p
            h = jax.nn.relu(xf @ w1e + b1e)
            y = h @ w2e + b2e
            return (acc + y * ce[:, None], None)
        acc0 = jnp.zeros_like(xf)
        out, _ = jax.lax.scan(body, acc0, (w1, b1, w2, b2, combine.T))
        return out.reshape(Bb, Ss, Hh)
    x = _layernorm(x + _L0_attn_ref(x, L0_attn_w_q, L0_attn_w_k, L0_attn_w_v, L0_attn_w_o), axis=-1)
    x = _layernorm(x + _L0_xattn_ref(x, ctx_1024, ctx_1024, L0_xattn_Wq, L0_xattn_bq, L0_xattn_Wk, L0_xattn_bk, L0_xattn_Wv, L0_xattn_bv), axis=-1)
    x = _layernorm(x + _L0_ffn_ref(x, L0_ffn_gate_w, L0_ffn_gate_b, L0_ffn_w1, L0_ffn_b1, L0_ffn_w2, L0_ffn_b2), axis=-1)
    return x

_drawn_inputs = setup_inputs


def setup_inputs(seed=0):
    import zlib

    import numpy as np

    out = dict(_drawn_inputs(seed))
    spreads = {'L0_xattn_bq': (0.0, 0.1),
     'L0_xattn_bk': (0.0, 0.8),
     'L0_xattn_bv': (0.0, 0.1),
     'L0_ffn_gate_b': (0.0, 0.1),
     'L0_ffn_b1': (0.0, 0.1),
     'L0_ffn_b2': (0.0, 0.1)}
    factors = {'L0_attn_w_q': 8.0, 'L0_attn_w_k': 7.082, 'L0_attn_w_v': 3.494, 'L0_attn_w_o': 4.366}
    for name, (base, spread) in spreads.items():
        noise = np.random.default_rng([zlib.crc32(name.encode()), seed]).standard_normal(out[name].shape)
        drawn = base * np.exp(spread * noise) if base else spread * noise
        out[name] = jnp.asarray(drawn.astype(out[name].dtype))
    for name, factor in factors.items():
        out[name] = (out[name] * factor).astype(out[name].dtype)
    return out
```

```python
from contextlib import ExitStack

import numpy as np

import concourse.bass as bass
from concourse import mybir

F32, BF16 = mybir.dt.float32, mybir.dt.bfloat16
I32, U32 = mybir.dt.int32, mybir.dt.uint32
ALU, ACT, AX = mybir.AluOpType, mybir.ActivationFunctionType, mybir.AxisListType

P = 128
B, S, D = 4, 1024, 256
C = 77
H, HD = 16, 16
NE, F = 8, 1024
KD = D // P
TB = S // P
NT = B * TB
FT = F // P
NH = B * H
EPS = 1e-5

Q_PARTS = "hhhmml"
K_PARTS = "hmlhmh"
STACK = 16 * len(Q_PARTS)
FULL = STACK + 3

ROWS_E = B * S + P
FFN_TILES = 2 * NT + NE
SPARE = FFN_TILES - 2 * NT
X_ROWS = NE * ROWS_E + SPARE * P
PAYLOAD = 260
Y_ROWS = 2 * B * S + (NE + SPARE) * P


class Shared:
    pass


class Ticks:

    def __init__(self, sem, per=0, by=1, credit=0):
        self.sem, self.per, self.by, self.credit = sem, per, by, credit

    def value(self, it, k):
        return it * (self.per * self.by) + (k + self.credit) * self.by

    def wait(self, eng, it, k):
        v = self.value(it, k)
        if isinstance(v, int) and v <= 0:
            return
        eng.wait_ge(self.sem, v)


class Line:

    def __init__(self, sem, order, credit=True):
        self.sem, self.order = sem, order
        self.index = {name: i for i, name in enumerate(order)}
        self.per = len(order)
        self.credit = self.per if credit else 0

    def wait(self, eng, it, name, ago=0):
        v = it * self.per + (self.index[name] + 1 + self.credit - ago * self.per)
        if isinstance(v, int) and v <= 0:
            return
        eng.wait_ge(self.sem, v)

    def begin(self, eng):
        if self.credit:
            eng.sem_inc(self.sem, self.credit)

    def emit(self, it, ops, skip=lambda name: False):
        for name in self.order:
            if not skip(name):
                ops[name[0]](it, *name[1:]).then_inc(self.sem, 1)


def settle(eng, sem):
    eng.sem_inc(sem, 1)


def build_program(nc, x, xT, wqT, wkT, wvT, woT, ctxT, cWqT, cbq, cWk, cbk, cWv, cbv,
                  gate_w, gate_b, w1, b1T, w2, b2, eye, lower, steps, out):
    g = Shared()
    g.x, g.xT, g.wqT, g.wkT, g.wvT, g.woT = x, xT, wqT, wkT, wvT, woT
    g.ctxT, g.cWqT, g.cbq, g.cWk, g.cbk, g.cWv = ctxT, cWqT, cbq, cWk, cbk, cWv
    g.cbv, g.gate_w, g.gate_b, g.w1, g.b1T, g.w2 = cbv, gate_w, gate_b, w1, b1T, w2
    g.b2, g.eye, g.lower, g.steps, g.out = b2, eye, lower, steps, out
    g.q_dram = nc.dram_tensor("q_stacks", [NH, STACK, S], BF16).ap()
    g.k_dram = nc.dram_tensor("k_stacks", [NH, STACK, S], BF16).ap()
    g.xe_dram = nc.dram_tensor("x_by_expert", [X_ROWS, PAYLOAD], F32).ap()
    g.ye_dram = nc.dram_tensor("y_by_token", [Y_ROWS, D], F32).ap()
    g.x2_dram = nc.dram_tensor("x2", [B * S, D], F32).ap()

    with ExitStack() as st:
        def sb(n, s, d=F32): return st.enter_context(nc.sbuf_tensor(n, s, d))
        def sem(n, **kw): return Ticks(st.enter_context(nc.semaphore(n)), **kw)

        g.ident = sb("ident", [P, P])
        g.ident_b = sb("ident_b", [P, P], BF16)
        g.below = sb("below", [P, P])
        g.ones = sb("ones", [P, P])
        g.step_c = sb("step_c", [P, steps.shape[1]])
        g.c_sum = sb("c_weights", [P, 2, NT])
        g.run = sb("run", [P, NE])
        g.gate_sb = sb("gate_w_sb", [P, KD, NE])
        g.gate_b_sb = sb("gate_b_sb", [1, NE])
        g.woT_sb = sb("woT_sb", [P, KD, D])
        g.b1_sb = sb("b1T_sb", [P, NE * FT])
        g.fold = sb("fold", [P, KD, B * C])
        g.fold_b = sb("fold_b", [1, B * C])
        g.cv = sb("cv", [C, B, D])
        g.neg_half = sb("neg_half", [P, TB])
        g.w1_sb = sb("w1_sb", [P, NE, KD, F])
        g.table = sb("table", [P, 2, FFN_TILES], I32)
        g.attn = sb("attn", [P, NH, TB, HD])

        g.w1_in = sem("w1_in", by=16)
        g.w2_in = sem("w2_in", by=16)
        g.const_in = sem("const_in", by=16)
        g.made = sem("constants_made")
        g.settled = sem("settled").sem
        g.col = {}
        at = 0
        for name, n in (("iota8", NE), ("region", NE), ("tiles", FFN_TILES), ("token", NT),
                        ("pads", NE + SPARE)):
            g.col[name] = slice(at, at + n)
            at += n

        with nc.sbuf_tensor("v_all", [P, NH, TB, HD], F32) as g.v_all:
            project(nc, g)
            attend(nc, g)
        with nc.sbuf_tensor("w2_sb", [P, NE, FT, D], F32) as g.w2_sb:
            norm_route(nc, g)
            experts(nc, g)
        combine(nc, g)


def project(nc, g):
    with ExitStack() as st:
        def sb(n, s, d=F32): return st.enter_context(nc.sbuf_tensor(n, s, d))
        def ps(n, s, d=F32): return st.enter_context(nc.psum_tensor(n, s, d))
        def sem(n, **kw): return Ticks(st.enter_context(nc.semaphore(n)), **kw)

        CH = 512
        NC = S // CH
        U = 2
        w_qk = sb("w_qk", [P, 2, KD, D])
        w_v = sb("w_v", [P, KD, D])
        xs = sb("xs", [P, U, KD, S])
        part = sb("part", [P, 4, 3, S], BF16)
        rest = sb("rest", [P, 4, CH])
        c_x = sb("c_x", [P, KD, B * C])
        c_w = sb("c_w", [P, 3, KD, D])
        c_bk = sb("c_bk", [P, KD])
        c_bq = sb("c_bq", [P, KD])
        c_bv = sb("c_bv", [1, D])
        c_k = sb("c_k", [P, KD, B * C])
        pq = [ps(f"pq{i}", [P, CH]) for i in range(4)]
        pv = [ps(f"pv{i}", [P, CH]) for i in range(2)]
        pc = [ps(f"pc{i}", [P, CH]) for i in range(2)]

        qk_in = sem("qk_in", by=16)
        v_in = sem("v_in", by=16)
        cross_in = sem("cross_in", by=16)
        x_in = [sem(f"x_in{u}", per=1, by=16 * KD) for u in range(U)]
        NQ = 4 * NC
        NV = TB // 2
        qk_done = sem("qk_done", per=U * NQ, credit=U * NQ)
        v_done = sem("v_done", per=U * NV, credit=U * NV)
        h_done = sem("h_done", per=U * NQ, credit=U * NQ)
        rest_done = sem("rest_done", per=U * NQ, credit=U * NQ)
        m_done = sem("m_done", per=U * NQ, credit=U * NQ)
        l_done = sem("l_done", per=U * NQ, credit=U * NQ)
        v_out = sem("v_out", per=U * NV, credit=U * NV)
        stored = [sem(f"stored{i}", per=U, by=16 * len(Q_PARTS), credit=U) for i in range(4)]
        cross_mm = sem("cross_mm")
        cross_k = sem("cross_k")
        cross_out = sem("cross_out")

        with nc.Block() as block:
            @block.sync
            def _(sp):
                sp.dma_start(w_qk[:, 0], g.wqT.rearrange("(k p) n -> p k n", p=P)).then_inc(qk_in.sem, 16)
                sp.dma_start(w_qk[:, 1], g.wkT.rearrange("(k p) n -> p k n", p=P)).then_inc(qk_in.sem, 16)
                sp.dma_start(w_v[:, :, :], g.wvT.rearrange("(k p) n -> p k n", p=P)).then_inc(v_in.sem, 16)
                for i in range(4):
                    sp.sem_inc(stored[i].sem, stored[i].value(0, 0))
                with sp.Fori(0, B // U) as it:
                    for u in range(U):
                        for j in range(4):
                            which, m = divmod(j, KD)
                            l_done.wait(sp, it, u * NQ + NC * (j + 1))
                            order, dst = ((Q_PARTS, g.q_dram), (K_PARTS, g.k_dram))[which]
                            head = (it * U + u) * H + m * (H // KD)
                            for r, name in enumerate(order):
                                sp.dma_start(dst[bass.ds(head, H // KD), 16 * r:16 * r + 16, :],
                                             part[:, j, "hml".index(name), :]).then_inc(stored[j].sem, 16)
                for i in range(4):
                    stored[i].wait(sp, B // U - 1, U)

            @block.scalar
            def _(act):
                act.dma_start(g.ident[:, :], g.eye).then_inc(g.const_in.sem, 16)
                act.dma_start(g.below[:, :], g.lower).then_inc(g.const_in.sem, 16)
                act.dma_start(g.step_c[:, :], g.steps).then_inc(g.const_in.sem, 16)
                act.dma_start(g.gate_sb[:, :, :], g.gate_w.rearrange("(k p) n -> p k n", p=P)).then_inc(g.const_in.sem, 16)
                act.dma_start(g.gate_b_sb[:, :], g.gate_b.rearrange("(a n) -> a n", a=1)).then_inc(g.const_in.sem, 16)
                act.dma_start(g.woT_sb[:, :, :], g.woT.rearrange("(k p) n -> p k n", p=P)).then_inc(g.const_in.sem, 16)
                act.dma_start(g.b1_sb[:, :], g.b1T).then_inc(g.const_in.sem, 16)
                act.dma_start(c_x[:, :, :], g.ctxT.rearrange("(k p) n -> p k n", p=P)).then_inc(cross_in.sem, 16)
                for i, w in enumerate((g.cWk, g.cWqT, g.cWv)):
                    act.dma_start(c_w[:, i], w.rearrange("(k p) n -> p k n", p=P)).then_inc(cross_in.sem, 16)
                act.dma_start(c_bk[:, :], g.cbk).then_inc(cross_in.sem, 16)
                act.dma_start(c_bq[:, :], g.cbq).then_inc(cross_in.sem, 16)
                act.dma_start(c_bv[:, :], g.cbv.rearrange("(a n) -> a n", a=1)).then_inc(cross_in.sem, 16)
                act.sem_inc(h_done.sem, U * NQ)
                act.sem_inc(m_done.sem, U * NQ)
                act.sem_inc(v_out.sem, U * NV)
                with act.Fori(0, B // U) as it:
                    def parts_h(i):
                        u, j, c = i // NQ, i // NC % 4, i % NC
                        qk_done.wait(act, it, i + 1)
                        stored[j].wait(act, it, u)
                        act.copy(part[:, j, 0, c * CH:(c + 1) * CH], pq[i % 4][:, :]).then_inc(h_done.sem, 1)

                    def parts_m(i):
                        j, c = i // NC % 4, i % NC
                        rest_done.wait(act, it, i + 1)
                        act.copy(part[:, j, 1, c * CH:(c + 1) * CH], rest[:, i % 4, :]).then_inc(m_done.sem, 1)

                    def take_v(n):
                        u, pair = divmod(n, NV)
                        v_done.wait(act, it, n + 1)
                        tile = pv[n % 2][:, :].rearrange("p (t h d) -> p t h d", t=2, h=H)
                        for t in range(2):
                            ins = act.copy(g.v_all[:, bass.ds((it * U + u) * H, H), 2 * pair + t, :], tile[:, t])
                        ins.then_inc(v_out.sem, 1)

                    for u in range(U):
                        for i in range(u * NQ, (u + 1) * NQ):
                            parts_h(i)
                            if i:
                                parts_m(i - 1)
                        for n in range(u * NV, (u + 1) * NV):
                            take_v(n)
                    parts_m(U * NQ - 1)
                for m in range(KD):
                    cross_mm.wait(act, 0, m + 1)
                    cross_in.wait(act, 0, 7)
                    act.activation(c_k[:, m, :], pc[m][:, 0:B * C], ACT.Identity, bias=c_bk[:, m:m + 1]
                                   ).then_inc(cross_k.sem, 1)

            @block.vector
            def _(dve):
                dve.sem_inc(rest_done.sem, U * NQ)
                dve.sem_inc(l_done.sem, U * NQ)
                dve.memset(g.ones[:, :], 1.0).then_inc(g.made.sem, 1)
                dve.memset(g.run[:, :], 0.0).then_inc(g.made.sem, 1)
                dve.memset(g.neg_half[:, :], -0.5).then_inc(g.made.sem, 1)
                g.const_in.wait(dve, 0, 7)
                dve.tensor_copy(g.ident_b[:, :], g.ident[:, :]).then_inc(g.made.sem, 1)
                with dve.Fori(0, B // U) as it:
                    def parts_l(i):
                        at = i // NC % 4, slice(i % NC * CH, (i % NC + 1) * CH)
                        m_done.wait(dve, it, i + 1)
                        dve.tensor_tensor(part[:, at[0], 2, at[1]], rest[:, i % 4, :], part[:, at[0], 1, at[1]],
                                          ALU.subtract).then_inc(l_done.sem, 1)

                    for i in range(U * NQ):
                        at = i // NC % 4, slice(i % NC * CH, (i % NC + 1) * CH)
                        h_done.wait(dve, it, i + 1)
                        l_done.wait(dve, it, i - 3)
                        dve.tensor_tensor(rest[:, i % 4, :], pq[i % 4][:, :], part[:, at[0], 0, at[1]],
                                          ALU.subtract).then_inc(rest_done.sem, 1)
                        if i:
                            parts_l(i - 1)
                    parts_l(U * NQ - 1)
                for m in range(KD):
                    cross_mm.wait(dve, 0, KD + 1 + m)
                    dve.tensor_copy(g.fold[:, m, :], pc[m][:, 0:B * C]).then_inc(cross_out.sem, 1)
                cross_mm.wait(dve, 0, 2 * KD + 1)
                dve.tensor_copy(g.fold_b[:, :], pv[0][0:1, 0:B * C]).then_inc(cross_out.sem, 1)
                for b in range(B):
                    cross_mm.wait(dve, 0, 2 * KD + 2 + b)
                    dve.tensor_copy(g.cv[:, b, :], pq[b][0:C, 0:D]).then_inc(cross_out.sem, 1)

            @block.gpsimd
            def _(pool):
                with pool.Fori(0, B // U) as it:
                    for u in range(U):
                        qk_done.wait(pool, it, (u + 1) * NQ - U * NQ)
                        v_done.wait(pool, it, (u + 1) * NV - U * NV)
                        for k in range(KD):
                            pool.dma_start(xs[:, u, k, :], g.xT[k * P:(k + 1) * P, bass.ds((it * U + u) * S, S)]
                                           ).then_inc(x_in[u].sem, 16)

            @block.tensor
            def _(pe):
                pe.sem_inc(qk_done.sem, U * NQ)
                pe.sem_inc(v_done.sem, U * NV)
                qk_in.wait(pe, 0, 2)
                v_in.wait(pe, 0, 1)
                with pe.Fori(0, B // U) as it:
                    for u in range(U):
                        x_in[u].wait(pe, it, 1)
                        for i in range(u * NQ, (u + 1) * NQ):
                            w, m, c = i // NC // KD % 2, i // NC % KD, i % NC
                            rest_done.wait(pe, it, i - 3)
                            for k in range(KD):
                                mm = pe.matmul(pq[i % 4][:, :], w_qk[:, w, k, m * P:(m + 1) * P],
                                               xs[:, u, k, c * CH:(c + 1) * CH], start=k == 0, stop=k == KD - 1)
                            mm.then_inc(qk_done.sem, 1)
                        for n in range(u * NV, (u + 1) * NV):
                            v_out.wait(pe, it, n - 1)
                            for t in range(2):
                                tok = (2 * (n % NV) + t) * P
                                for k in range(KD):
                                    mm = pe.matmul(pv[n % 2][:, t * D:(t + 1) * D], xs[:, u, k, tok:tok + P],
                                                   w_v[:, k, :], start=k == 0, stop=k == KD - 1)
                            mm.then_inc(v_done.sem, 1)
                cross_in.wait(pe, 0, 7)
                for m in range(KD):
                    for k in range(KD):
                        mm = pe.matmul(pc[m][:, 0:B * C], c_w[:, 0, k, m * P:(m + 1) * P], c_x[:, k, :],
                                       start=k == 0, stop=k == KD - 1)
                    mm.then_inc(cross_mm.sem, 1)
                for m in range(KD):
                    cross_k.wait(pe, 0, KD)
                    for k in range(KD):
                        mm = pe.matmul(pc[m][:, 0:B * C], c_w[:, 1, k, m * P:(m + 1) * P], c_k[:, k, :],
                                       start=k == 0, stop=k == KD - 1)
                    mm.then_inc(cross_mm.sem, 1)
                v_out.wait(pe, B // U - 1, U * NV)
                for k in range(KD):
                    mm = pe.matmul(pv[0][0:1, 0:B * C], c_bq[:, k:k + 1], c_k[:, k, :],
                                   start=k == 0, stop=k == KD - 1)
                mm.then_inc(cross_mm.sem, 1)
                rest_done.wait(pe, B // U - 1, U * NQ)
                g.made.wait(pe, 0, 4)
                for b in range(B):
                    for k in range(KD):
                        pe.matmul(pq[b][0:C, 0:D], c_x[:, k, b * C:(b + 1) * C], c_w[:, 2, k, :],
                                  start=k == 0, stop=False)
                    pe.matmul(pq[b][0:C, 0:D], g.ones[0:1, 0:C], c_bv[:, :],
                              start=False, stop=True).then_inc(cross_mm.sem, 1)


def attend(nc, g):
    LEAD = 14
    U = 4
    UN = U * TB
    IT = NH // U
    HALF = S // 2
    SCALE = float(HD) ** -0.5
    VW = 32
    with ExitStack() as st:
        def sb(n, s, d=F32): return st.enter_context(nc.sbuf_tensor(n, s, d))
        def ps(n, s, d=F32): return st.enter_context(nc.psum_tensor(n, s, d))
        def sem(n, **kw): return Ticks(st.enter_context(nc.semaphore(n)), **kw)

        qs = [sb(f"qs{i}", [FULL, S], BF16) for i in range(U)]
        ks = [sb(f"ks{i}", [FULL, S], BF16) for i in range(U)]
        vs = [sb(f"vs{i}", [P, TB, VW]) for i in range(2)]
        ex = [sb(f"ex{i}", [P, S]) for i in range(4)]
        o_sb = [sb(f"o_sb{i}", [P, D]) for i in range(2)]
        mx = [sb(f"mx{i}", [P, TB]) for i in range(2)]
        neg = sb("neg", [P, TB])
        left = sb("left", [P, TB])
        minus = sb("minus", [P, TB])
        neg_parts = [sb(f"neg_parts{i}", [P, 3, TB], BF16) for i in range(2)]
        neg_rows = [sb(f"neg_rows{i}", [3 * TB, P], BF16) for i in range(2)]
        rec = [sb(f"rec{i}", [P, TB]) for i in range(2)]
        pa = [ps(f"pa{i}", [P, S]) for i in range(2)]
        pb = [ps(f"pb{i}", [P, HALF]) for i in range(2)]
        po = [ps(f"po{i}", [P, HALF]) for i in range(2)]

        loaded = [sem(f"loaded{i}", per=1, by=32) for i in range(U)]
        rows_in = [sem(f"rows_in{i}", per=1, by=16) for i in range(U)]
        a_done = sem("a_done", per=UN)
        max_done = sem("max_done", per=UN)
        POOL_OPS = 6
        pool_step = sem("pool_step", per=POOL_OPS * U)
        parts_t = sem("parts_t", per=U)
        parts_out = sem("parts_out", per=U)
        b_done = sem("b_done", per=2 * UN)
        e_done = sem("e_done", per=2 * UN)
        pv_done = sem("pv_done", per=UN)
        o_out = sem("o_out", per=U)
        o_t = sem("o_t", per=U)
        rec_done = sem("rec_done", per=U)
        norm_done = sem("norm_done", per=U)
        set_up = sem("set_up")

        def over(eng, body):
            body(0)
            with eng.Fori(1, IT - 1) as it:
                body(it)
            body(IT - 1)

        def there(it, i):
            return not isinstance(it, int) or 0 <= it * U + i < NH

        with nc.Block() as block:
            @block.sync
            def _(sp):
                sp.dma_start(g.w1_sb[:, :, :, :].rearrange("p e k f -> p (e k) f"),
                             g.w1.rearrange("e (k p) f -> p (e k) f", p=P)).then_inc(g.w1_in.sem, 16)

                def load(it, i):
                    b_done.wait(sp, it, 2 * TB * (i - U + 1))
                    head = it * U + i
                    sp.dma_start(qs[i % U][0:STACK, :], g.q_dram[bass.ds(head, 1)].rearrange("h r t -> (h r) t")
                                 ).then_inc(loaded[i % U].sem, 16)
                    sp.dma_start(ks[i % U][0:STACK, :], g.k_dram[bass.ds(head, 1)].rearrange("h r t -> (h r) t")
                                 ).then_inc(loaded[i % U].sem, 16)

                def rows(it, i):
                    parts_out.wait(sp, it, i + 1)
                    sp.dma_start(qs[i % U][STACK:FULL, :], neg_rows[i % 2][:, :]).then_inc(rows_in[i % U].sem, 16)

                for i in range(3):
                    load(0, i)
                rows(0, 0)

                def body(it):
                    for i in range(U):
                        if there(it, i + 3):
                            load(it, i + 3)
                        if there(it, i + 1):
                            rows(it, i + 1)
                over(sp, body)

            @block.gpsimd
            def _(pool):
                one = g.ones[:, :]
                set_up.wait(pool, 0, U + 3)
                g.made.wait(pool, 0, 4)

                def chain(it, i, j, op):
                    pool_step.wait(pool, it, POOL_OPS * i + j)
                    op().then_inc(pool_step.sem, 1)

                def values(it, i):
                    pv_done.wait(pool, it, TB * (i - 1))
                    chain(it, i, 0, lambda: pool.tensor_tensor(
                        vs[i % 2][:, :, 0:HD], g.v_all[:, bass.ds(it * U + i, 1)].rearrange("p h t d -> p (h t) d"),
                        one.rearrange("p (t d) -> p t d", t=TB), ALU.mult))

                def split(it, i):
                    max_done.wait(pool, it, TB * (i + 1))
                    parts_t.wait(pool, it, i - 1)
                    dst, src = neg_parts[i % 2], mx[i % 2][:, :]
                    chain(it, i, 1, lambda: pool.tensor_tensor(neg[:, :], src, minus[:, :], ALU.mult))
                    chain(it, i, 2, lambda: pool.tensor_tensor(dst[:, 0, :], neg[:, :], one[:, 0:TB], ALU.mult))
                    chain(it, i, 3, lambda: pool.tensor_tensor(left[:, :], neg[:, :], dst[:, 0, :], ALU.subtract))
                    chain(it, i, 4, lambda: pool.tensor_tensor(dst[:, 1, :], left[:, :], one[:, 0:TB], ALU.mult))
                    chain(it, i, 5, lambda: pool.tensor_tensor(dst[:, 2, :], left[:, :], dst[:, 1, :], ALU.subtract))

                values(0, 0)
                split(0, 0)

                def body(it):
                    for i in range(U):
                        if there(it, i + 1):
                            values(it, i + 1)
                            split(it, i + 1)
                over(pool, body)

            @block.tensor
            def _(pe):
                def score_max(it, n):
                    i, t = divmod(n, TB)
                    if t == 0:
                        loaded[i % U].wait(pe, it, i // U + 1)
                    max_done.wait(pe, it, n - 1)
                    for half in range(2):
                        mm = pe.matmul(pa[n % 2][:, half * HALF:(half + 1) * HALF],
                                       qs[i % U][0:STACK, t * P:(t + 1) * P],
                                       ks[i % U][0:STACK, half * HALF:(half + 1) * HALF], start=True, stop=True)
                    mm.then_inc(a_done.sem, 1)

                def score_exp(it, n):
                    i, t = divmod(n, TB)
                    if t == 0:
                        rows_in[i % U].wait(pe, it, i // U + 1)
                    for half in range(2):
                        e_done.wait(pe, it, 2 * n - 1 + half)
                        pe.matmul(pb[half][:, :], ks[i % U][:, t * P:(t + 1) * P],
                                  qs[i % U][:, half * HALF:(half + 1) * HALF], start=True, stop=True
                                  ).then_inc(b_done.sem, 1)

                def values(it, n):
                    i, t = divmod(n, TB)
                    if t == 0:
                        pool_step.wait(pe, it, POOL_OPS * i + 1)
                        norm_done.wait(pe, it, i - 1)
                        parts_out.wait(pe, it, i + 1)
                    e_done.wait(pe, it, 2 * n + 2)
                    for j in range(4):
                        mm = pe.matmul(po[i % 2][32 * j:32 * j + VW, 0:D], vs[i % 2][:, t, :],
                                       ex[n % 4][:, j * D:(j + 1) * D], start=t == 0, stop=t == TB - 1,
                                       tile_position=(0, 32 * j))
                    mm.then_inc(pv_done.sem, 1)

                def turn_output(it, i):
                    o_out.wait(pe, it, i + 1)
                    for t in range(2):
                        mm = pe.transpose(po[i % 2][:, D + t * P:D + (t + 1) * P], o_sb[i % 2][:, t * P:(t + 1) * P],
                                          g.ident[:, :])
                    mm.then_inc(o_t.sem, 1)

                def turn_parts(it, i):
                    pool_step.wait(pe, it, POOL_OPS * (i + 1))
                    norm_done.wait(pe, it, i - 1)
                    pe.transpose(po[i % 2][0:3 * TB, 0:P // 2].bitcast(BF16),
                                 neg_parts[i % 2][:, :, :].rearrange("p a t -> p (a t)"), g.ident_b[:, :]
                                 ).then_inc(parts_t.sem, 1)

                g.const_in.wait(pe, 0, 7)
                g.made.wait(pe, 0, 4)
                set_up.wait(pe, 0, U + 2)
                for n in range(TB):
                    score_max(0, n)
                turn_parts(0, 0)
                for n in range(TB, LEAD):
                    score_max(0, n)
                score_exp(0, 0)

                def body(it):
                    for n in range(UN):
                        i, t = divmod(n, TB)
                        if t == 2 and there(it, i - 1):
                            turn_output(it, i - 1)
                        if t == 5 and there(it, i + 1):
                            turn_parts(it, i + 1)
                        if there(it, (n + 1) // TB):
                            score_exp(it, n + 1)
                        values(it, n)
                        if there(it, (n + LEAD) // TB):
                            score_max(it, n + LEAD)
                over(pe, body)
                turn_output(IT, -1)

            @block.scalar
            def _(act):
                def exponentials(it, n):
                    for half in range(2):
                        b_done.wait(act, it, 2 * n + 1 + half)
                        if half == 0:
                            pv_done.wait(act, it, n - 3)
                        act.activation(ex[n % 4][:, half * HALF:(half + 1) * HALF], pb[half][:, :], ACT.Exp,
                                       scale=SCALE).then_inc(e_done.sem, 1)

                def take_output(it, i):
                    pv_done.wait(act, it, TB * (i + 1))
                    o_t.wait(act, it, i - 1)
                    act.copy(o_sb[i % 2][:, :], po[i % 2][:, 0:D]).then_inc(o_out.sem, 1)

                def take_parts(it, i):
                    parts_t.wait(act, it, i + 1)
                    rows_in[(i - 2) % U].wait(act, it, (i - 2) // U + 1)
                    act.copy(neg_rows[i % 2][:, :], po[i % 2][0:3 * TB, 0:P // 2].bitcast(BF16)).then_inc(parts_out.sem, 1)

                take_parts(0, 0)

                def body(it):
                    for n in range(UN):
                        i, t = divmod(n, TB)
                        exponentials(it, n)
                        if t == 0 and there(it, i - 1):
                            take_output(it, i - 1)
                        if t == 5 and there(it, i + 1):
                            take_parts(it, i + 1)
                over(act, body)
                take_output(IT, -1)

            @block.vector
            def _(dve):
                def maxima(it, n):
                    i, t = divmod(n, TB)
                    if t == 0:
                        pool_step.wait(dve, it, POOL_OPS * (i - 1))
                    a_done.wait(dve, it, n + 1)
                    dve.tensor_reduce(mx[i % 2][:, t:t + 1], pa[n % 2][:, :], AX.X, ALU.max).then_inc(max_done.sem, 1)

                def normalise(it, i):
                    o_t.wait(dve, it, i + 1)
                    tile = po[i % 2][:, D:2 * D].rearrange("p (t j d) -> p t j d", t=2, j=4)
                    r = rec[i % 2][:, :].rearrange("p (j t) -> p t j", j=4)
                    dve.reciprocal(r, tile[:, :, :, HD]).then_inc(rec_done.sem, 1)
                    rec_done.wait(dve, it, i + 1)
                    dst = g.attn[:, bass.ds(it * U + i, 1)].rearrange("p h (j t) d -> p t (h j) d", j=4)
                    dve.tensor_tensor(dst, tile[:, :, :, 0:HD],
                                      r.rearrange("p t (j o) -> p t j o", o=1).to_broadcast([P, 2, 4, HD]),
                                      ALU.mult).then_inc(norm_done.sem, 1)

                for i in range(U):
                    dve.memset(ks[i][STACK:FULL, :], 1.0).then_inc(set_up.sem, 1)
                for i in range(2):
                    dve.memset(vs[i][:, :, HD:VW], 1.0).then_inc(set_up.sem, 1)
                dve.memset(minus[:, :], -1.0).then_inc(set_up.sem, 1)
                for n in range(LEAD):
                    maxima(0, n)

                def body(it):
                    for n in range(UN):
                        i, t = divmod(n, TB)
                        if there(it, (n + LEAD) // TB):
                            maxima(it, n + LEAD)
                        if t == 3 and there(it, i - 1):
                            normalise(it, i - 1)
                over(dve, body)
                normalise(IT, -1)


def norm_route(nc, g):
    G = TB // 2
    BETA = D ** -0.5
    with ExitStack() as st:
        def sb(n, s, d=F32): return st.enter_context(nc.sbuf_tensor(n, s, d))
        def ps(n, s, d=F32): return st.enter_context(nc.psum_tensor(n, s, d))
        def sem(n): return st.enter_context(nc.semaphore(n))

        xt = sb("xt", [P, TB, D])
        pay = [sb(f"pay{i}", [P, TB, PAYLOAD]) for i in range(2)]
        at = [sb(f"at{i}", [P, D]) for i in range(2)]
        turned = [sb(f"turned{i}", [P, KD, P]) for i in range(2)]
        pr = [sb(f"pr{i}", [P, C]) for i in range(2)]
        prT = [sb(f"prT{i}", [C, P]) for i in range(2)]
        stats = sb("stats", [P, TB, 6])
        mv = sb("mv", [P, TB, 2])
        dev = sb("dev", [P, TB])
        rstd = sb("rstd", [P, TB])
        eps = sb("eps", [P, TB])
        cmax = sb("cmax", [P, TB])
        cneg = sb("cneg", [P, TB])
        csum = sb("csum", [P, TB])
        crec = sb("crec", [P, TB])
        lg = sb("lg", [P, TB, NE])
        top = sb("top", [P, TB, 8])
        top_i = sb("top_i", [P, TB, 8], U32)
        top_f = sb("top_f", [P, TB, 2])
        hot = [sb(f"hot{i}", [P, TB, NE]) for i in range(2)]
        both = sb("both", [P, TB, NE])
        gap = sb("gap", [P, TB])
        gap_e = sb("gap_e", [P, TB])
        base = sb("base", [P, TB + 1, NE])
        pos = sb("pos", [P, TB, NE])
        picked = sb("picked", [P, TB, NE])
        pos_f = sb("pos_f", [P, 2, TB])
        pos_i = sb("pos_i", [P, 2, TB], I32)
        pT = [ps(f"pT{i}", [P, KD, P]) for i in range(2)]
        pO = [ps(f"pO{i}", [P, D]) for i in range(2)]
        pS = [ps(f"pS{i}", [P, C]) for i in range(2)]
        pPT = ps("pPT", [C, P])
        pG = ps("pG", [P, 3, TB, NE])

        T = range(TB)

        def skewed(*kinds):
            last = max(lag for _, lag in kinds)
            return [(k, s - lag) for s in range(TB + last) for k, lag in kinds if 0 <= s - lag < TB]

        def after(names, anchor, more):
            i = names.index(anchor) + 1
            return names[:i] + more + names[i:]

        pe_l = Line(sem("nr_pe"), skewed(("turn_a", 0), ("proj", 1))
                    + skewed(("turn_1", 0), ("score", 1), ("turn_p", 3), ("cross", 4))
                    + skewed(("turn_2", 0), ("gate", 1)) + [("rank",), ("total",)])
        act_l = Line(sem("nr_act"), skewed(("gather", 0), ("copy_a", 1))
                     + skewed(("copy_1", 0), ("soft", 2), ("copy_p", 3))
                     + skewed(("copy_2", 0), ("second", 0)) + [("gap_exp",)])
        first = after(skewed(("add", 0), ("stat_1", 0), ("aggr_1", 1)), ("aggr_1", G), [("norm_1", t) for t in T[:G]])
        second = after(skewed(("max", 1), ("neg", 1), ("rec", 4), ("mix", 4), ("stat_2", 4), ("aggr_2", 5)),
                       ("aggr_2", G), [("norm_2", t) for t in T[:G]])
        dve_l = Line(sem("nr_dve"), first + [("norm_1", t) for t in T[G:]] + second + [("norm_2", t) for t in T[G:]]
                     + [("row", i) for i in range(2)] + [("logits",)]
                     + [("top", t) for t in T] + [("top_i", t) for t in T]
                     + [("top_f",), ("hot", 0), ("hot", 1), ("both",), ("gap",), ("base", 0)]
                     + [("base", t) for t in range(1, TB + 1)] + [("pos",), ("region",)]
                     + [("pick", 0), ("sum", 0), ("pick", 1), ("sum", 1), ("pos_i",)]
                     + [("one_plus",), ("w_first",), ("w_second",)])
        pool_l = Line(sem("nr_pool"), [(k, n, h) for n in (1, 2) for h in range(2) for k in ("var", "rstd")])
        x_in, scattered, x2_out = sem("nr_x_in"), sem("scattered"), sem("x2_out")
        payload_free, payload_left = sem("payload_free"), sem("payload_left")
        set_up, table_step, pads_in, spare_in = (sem(n) for n in ("nr_set_up", "table_step", "pads_in", "spare_in"))
        SC = 16 * 2 * TB

        with nc.Block() as block:
            @block.sync
            def _(sp):
                sp.dma_start(g.w2_sb[:, :, :, :].rearrange("p e f d -> p (e f) d"),
                             g.w2.rearrange("e (f p) d -> p (e f) d", p=P)).then_inc(g.w2_in.sem, 16)
                sp.sem_inc(x2_out, 16)
                with sp.Fori(0, B) as it:
                    dve_l.wait(sp, it, ("mix", TB - 1), ago=1)
                    sp.dma_start(xt[:, :, :], g.x.rearrange("(b t p) d -> p b t d", p=P, t=TB)
                                 [:, bass.ds(it, 1)].rearrange("p b t d -> p (b t) d")).then_inc(x_in, 16)
                    dve_l.wait(sp, it, ("norm_2", TB - 1))
                    sp.dma_start(g.x2_dram.rearrange("(b t p) d -> p b t d", p=P, t=TB)
                                 [:, bass.ds(it, 1)].rearrange("p b t d -> p (b t) d"), pay[0][:, :, 0:D]).then_inc(x2_out, 16)
                sp.wait_ge(x2_out, 16 * B + 16)
                sp.wait_ge(table_step, 2)
                at_row = NE * ROWS_E
                sp.dma_start(g.xe_dram[at_row:at_row + SPARE * P, :].rearrange("(k p) d -> p k d", p=P),
                             pay[1][:, 0:SPARE, :]).then_inc(spare_in, 16)
                sp.wait_ge(spare_in, 16)

            @block.tensor
            def _(pe):
                def turn(src, i, t):
                    for k in range(KD):
                        mm = pe.transpose(pT[i][:, k, :], src[:, k * P:(k + 1) * P], g.ident[:, :])
                    return mm

                def turn_a(it, t):
                    act_l.wait(pe, it, ("gather", t))
                    if t >= 2:
                        act_l.wait(pe, it, ("copy_a", t - 2))
                    return turn(at[t % 2], t % 2, t)

                def product(out, src, rhs, last=None):
                    for k in range(KD):
                        mm = pe.matmul(out, src[:, k, :], rhs(k), start=k == 0, stop=last is None and k == KD - 1)
                    if last:
                        mm = pe.matmul(out, g.ones[0:1, :], last, start=False, stop=True)
                    return mm

                def proj(it, t):
                    act_l.wait(pe, it, ("copy_a", t))
                    if t >= 2:
                        dve_l.wait(pe, it, ("add", t - 2))
                    return product(pO[t % 2][:, :], turned[t % 2], lambda k: g.woT_sb[:, k, :])

                def turn_1(it, t):
                    dve_l.wait(pe, it, ("norm_1", t))
                    act_l.wait(pe, it, ("copy_1", t - 2) if t >= 2 else ("copy_a", TB - 2 + t))
                    return turn(xt[:, t], t % 2, t)

                def score(it, t):
                    act_l.wait(pe, it, ("copy_1", t))
                    if t >= 2:
                        act_l.wait(pe, it, ("soft", t - 2))
                    return product(pS[t % 2][:, :], turned[t % 2], lambda k: g.fold[:, k, bass.ds(it * C, C)],
                                   g.fold_b[:, bass.ds(it * C, C)])

                def turn_p(it, t):
                    act_l.wait(pe, it, ("soft", t))
                    if t:
                        act_l.wait(pe, it, ("copy_p", t - 1))
                    return pe.transpose(pPT[:, :], pr[t % 2][:, :], g.ident[:, :])

                def cross(it, t):
                    act_l.wait(pe, it, ("copy_p", t))
                    dve_l.wait(pe, it, ("mix", t - 2) if t >= 2 else ("add", TB - 2 + t))
                    return pe.matmul(pO[t % 2][:, :], prT[t % 2][:, :],
                                     g.cv[:, bass.ds(it, 1), :].rearrange("c b d -> c (b d)"), start=True, stop=True)

                def turn_2(it, t):
                    dve_l.wait(pe, it, ("norm_2", t))
                    act_l.wait(pe, it, ("copy_2", t - 2) if t >= 2 else ("copy_1", TB - 2 + t))
                    return turn(pay[0][:, t], t % 2, t)

                def gate(it, t):
                    act_l.wait(pe, it, ("copy_2", t))
                    if t == 0:
                        dve_l.wait(pe, it, ("pos",), ago=1)
                    return product(pG[:, 0, t, :], turned[t % 2], lambda k: g.gate_sb[:, k, :], g.gate_b_sb[:, :])

                def rank(it):
                    dve_l.wait(pe, it, ("both",))
                    return pe.matmul(pG[:, 1].rearrange("p t e -> p (t e)"), g.below[:, :],
                                     both[:, :, :].rearrange("p t e -> p (t e)"), start=True, stop=True)

                def total(it):
                    return pe.matmul(pG[:, 2].rearrange("p t e -> p (t e)"), g.ones[:, :],
                                     both[:, :, :].rearrange("p t e -> p (t e)"), start=True, stop=True)

                pe_l.begin(pe)
                with pe.Fori(0, B) as it:
                    pe_l.emit(it, {"turn_a": turn_a, "proj": proj, "turn_1": turn_1, "score": score, "turn_p": turn_p,
                                   "cross": cross, "turn_2": turn_2, "gate": gate, "rank": rank, "total": total})

            @block.scalar
            def _(act):
                def gather(it, t):
                    pe_l.wait(act, it, ("turn_a", t - 2) if t >= 2 else ("turn_a", TB - 2 + t), ago=0 if t >= 2 else 1)
                    return act.copy(at[t % 2][:, :].rearrange("p (h d) -> p h d", h=H),
                                    g.attn[:, bass.ds(it * H, H), t, :])

                def take(t):
                    return act.copy(turned[t % 2][:, :, :], pT[t % 2][:, :, :])

                def copy_a(it, t):
                    pe_l.wait(act, it, ("turn_a", t))
                    pe_l.wait(act, it, ("proj", t - 2) if t >= 2 else ("gate", TB - 2 + t), ago=0 if t >= 2 else 1)
                    return take(t)

                def copy_1(it, t):
                    pe_l.wait(act, it, ("turn_1", t))
                    pe_l.wait(act, it, ("score", t - 2) if t >= 2 else ("proj", TB - 2 + t))
                    return take(t)

                def copy_2(it, t):
                    pe_l.wait(act, it, ("turn_2", t))
                    pe_l.wait(act, it, ("gate", t - 2) if t >= 2 else ("score", TB - 2 + t))
                    return take(t)

                def soft(it, t):
                    dve_l.wait(act, it, ("neg", t))
                    pe_l.wait(act, it, ("turn_p", t - 2) if t >= 2 else ("turn_p", TB - 2 + t), ago=0 if t >= 2 else 1)
                    return act.activation(pr[t % 2][:, :], pS[t % 2][:, :], ACT.Exp, scale=BETA,
                                          bias=cneg[:, t:t + 1], accum_out=csum[:, t:t + 1])

                def copy_p(it, t):
                    pe_l.wait(act, it, ("turn_p", t))
                    pe_l.wait(act, it, ("cross", t - 2) if t >= 2 else ("cross", TB - 2 + t), ago=0 if t >= 2 else 1)
                    return act.copy(prT[t % 2][:, :], pPT[:, :])

                def second(it, t):
                    dve_l.wait(act, it, ("norm_2", t))
                    if t == 0:
                        act.wait_ge(payload_free, it + 1)
                    return act.copy(pay[1][:, t, 0:D], pay[0][:, t, 0:D])

                def gap_exp(it):
                    dve_l.wait(act, it, ("gap",))
                    return act.activation(gap_e[:, :], gap[:, :], ACT.Exp)

                act_l.begin(act)
                with act.Fori(0, B) as it:
                    act_l.emit(it, {"gather": gather, "copy_a": copy_a, "copy_1": copy_1, "soft": soft,
                                    "copy_p": copy_p, "copy_2": copy_2, "second": second, "gap_exp": gap_exp})

            @block.vector
            def _(dve):
                def add(it, t):
                    pe_l.wait(dve, it, ("proj", t))
                    if t == 0:
                        dve.wait_ge(x_in, it * 16 + 16)
                    return dve.tensor_tensor(xt[:, t], pO[t % 2][:, :], xt[:, t], ALU.add)

                def stat(src, t):
                    return dve.bn_stats(stats[:, t, :], src)

                def stat_1(it, t):
                    dve_l.wait(dve, it, ("add", t))
                    return stat(xt[:, t], t)

                def aggr_1(it, t):
                    dve_l.wait(dve, it, ("stat_1", t))
                    if t == 0:
                        pool_l.wait(dve, it, ("rstd", 2, 1), ago=1)
                    settle(dve, g.settled)
                    return dve.bn_aggr(mv[:, t, :], stats[:, t, :])

                def normalise(it, n, t, dst, src):
                    pool_l.wait(dve, it, ("rstd", n, t // G))
                    return dve.tensor_scalar(dst, src, mv[:, t, 0:1], rstd[:, t:t + 1], ALU.subtract, ALU.mult)

                def norm_1(it, t):
                    return normalise(it, 1, t, xt[:, t], xt[:, t])

                def max_(it, t):
                    pe_l.wait(dve, it, ("score", t))
                    if t < 2:
                        act_l.wait(dve, it, ("soft", TB - 2 + t), ago=1)
                    return dve.tensor_reduce(cmax[:, t:t + 1], pS[t % 2][:, :], AX.X, ALU.max)

                def neg(it, t):
                    dve_l.wait(dve, it, ("max", t))
                    return dve.tensor_scalar(cneg[:, t:t + 1], cmax[:, t:t + 1], -BETA, None, ALU.mult)

                def rec(it, t):
                    act_l.wait(dve, it, ("soft", t))
                    return dve.reciprocal(crec[:, t:t + 1], csum[:, t:t + 1])

                def mix(it, t):
                    dve_l.wait(dve, it, ("rec", t))
                    pe_l.wait(dve, it, ("cross", t))
                    if t == 0:
                        dve.wait_ge(payload_free, it + 1)
                        dve.wait_ge(x2_out, it * 16 + 16)
                    return dve.scalar_tensor_tensor(pay[0][:, t, 0:D], pO[t % 2][:, :], crec[:, t:t + 1], xt[:, t],
                                                    ALU.mult, ALU.add)

                def stat_2(it, t):
                    dve_l.wait(dve, it, ("mix", t))
                    return stat(pay[0][:, t, 0:D], t)

                def aggr_2(it, t):
                    dve_l.wait(dve, it, ("stat_2", t))
                    settle(dve, g.settled)
                    return dve.bn_aggr(mv[:, t, :], stats[:, t, :])

                def norm_2(it, t):
                    return normalise(it, 2, t, pay[0][:, t, 0:D], pay[0][:, t, 0:D])

                def row(it, i):
                    return dve.tensor_scalar(pay[i][:, :, D].bitcast(I32), g.step_c[:, bass.ds(it * TB + g.col["token"].start, TB)],
                                             float(i), None, ALU.add)

                def logits(it):
                    pe_l.wait(dve, it, ("gate", TB - 1))
                    return dve.tensor_copy(lg[:, :, :], pG[:, 0])

                def top_(it, t):
                    if t == 0:
                        dve_l.wait(dve, it, ("logits",))
                        settle(dve, g.settled)
                    return dve.max(top[:, t, :], lg[:, t, :])

                def top_i_(it, t):
                    dve_l.wait(dve, it, ("top", t))
                    settle(dve, g.settled)
                    return dve.max_index(top_i[:, t, :], top[:, t, :], lg[:, t, :])

                def top_f_(it):
                    dve_l.wait(dve, it, ("top_i", TB - 1))
                    return dve.tensor_copy(top_f[:, :, :], top_i[:, :, 0:2])

                def by_expert(ap):
                    return ap.rearrange("p (t o) -> p t o", o=1).to_broadcast([P, TB, NE])

                def by_tile(ap):
                    return ap.rearrange("p (o e) -> p o e", o=1).to_broadcast([P, TB, NE])

                def hot_(it, i):
                    dve_l.wait(dve, it, ("top_f",))
                    return dve.tensor_tensor(hot[i][:, :, :], by_expert(top_f[:, :, i]), by_tile(g.step_c[:, g.col["iota8"]]),
                                             ALU.is_equal)

                def both_(it):
                    dve_l.wait(dve, it, ("hot", 1))
                    return dve.tensor_tensor(both[:, :, :], hot[0][:, :, :], hot[1][:, :, :], ALU.add)

                def gap_(it):
                    act_l.wait(dve, it, ("gap_exp",), ago=1)
                    return dve.tensor_tensor(gap[:, :], top[:, :, 1], top[:, :, 0], ALU.subtract)

                def base_(it, t):
                    if t == 0:
                        dve_l.wait(dve, it, ("base", TB), ago=1)
                        return dve.tensor_copy(base[:, 0, :], g.run[:, :])
                    pe_l.wait(dve, it, ("total",))
                    dve_l.wait(dve, it, ("base", t - 1))
                    dst = g.run[:, :] if t == TB else base[:, t, :]
                    return dve.tensor_tensor(dst, base[:, t - 1, :], pG[:, 2, t - 1, :], ALU.add)

                def pos_(it):
                    dve_l.wait(dve, it, ("base", TB))
                    return dve.tensor_tensor(pos[:, :, :], pG[:, 1], base[:, 0:TB, :], ALU.add)

                def region(it):
                    dve_l.wait(dve, it, ("pos",))
                    return dve.tensor_tensor(pos[:, :, :], pos[:, :, :], by_tile(g.step_c[:, g.col["region"]]), ALU.add)

                def pick(it, i):
                    dve_l.wait(dve, it, ("sum", 0) if i else ("region",))
                    return dve.tensor_tensor(picked[:, :, :], pos[:, :, :], hot[i][:, :, :], ALU.mult)

                def sum_(it, i):
                    dve_l.wait(dve, it, ("pick", i))
                    return dve.tensor_reduce(pos_f[:, i, :], picked[:, :, :], AX.X, ALU.add)

                def pos_i_(it):
                    dve_l.wait(dve, it, ("sum", 1))
                    return dve.tensor_copy(pos_i[:, :, :], pos_f[:, :, :])

                def weights(i, it):
                    return g.c_sum[:, i, bass.ds(it * TB, TB)]

                def one_plus(it):
                    act_l.wait(dve, it, ("gap_exp",))
                    return dve.tensor_scalar(gap[:, :], gap_e[:, :], 1.0, None, ALU.add)

                def w_first(it):
                    dve_l.wait(dve, it, ("one_plus",))
                    return dve.reciprocal(weights(0, it), gap[:, :])

                def w_second(it):
                    dve_l.wait(dve, it, ("w_first",))
                    return dve.tensor_tensor(weights(1, it), gap_e[:, :], weights(0, it), ALU.mult)

                ops = {"add": add, "stat_1": stat_1, "aggr_1": aggr_1, "norm_1": norm_1, "max": max_, "neg": neg,
                       "rec": rec, "mix": mix, "stat_2": stat_2, "aggr_2": aggr_2, "norm_2": norm_2, "row": row,
                       "logits": logits, "top": top_, "top_i": top_i_, "top_f": top_f_, "hot": hot_, "both": both_,
                       "gap": gap_, "base": base_, "pos": pos_, "region": region, "pick": pick, "sum": sum_,
                       "pos_i": pos_i_, "one_plus": one_plus, "w_first": w_first, "w_second": w_second}
                dve_l.begin(dve)
                dve.memset(eps[:, :], EPS).then_inc(set_up, 1)
                for i in range(2):
                    dve.memset(pay[i][:, :, D:PAYLOAD], 0.0).then_inc(set_up, 1)
                dve.wait_ge(set_up, 3)
                with dve.Fori(0, B) as it:
                    dve_l.emit(it, ops)
                dve.wait_ge(payload_free, B + 1)
                dve.wait_ge(x2_out, 16 * B + 16)
                tile_table(nc, dve, g, st, pay, pos_i, xt, table_step)

            @block.gpsimd
            def _(pool):
                def var(it, n, h):
                    dve_l.wait(pool, it, (f"aggr_{n}", h * G + G - 1))
                    return pool.tensor_tensor(dev[:, h * G:h * G + G], mv[:, h * G:h * G + G, 1], eps[:, 0:G], ALU.add)

                def rstd_(it, n, h):
                    pool_l.wait(pool, it, ("var", n, h))
                    return pool.tensor_tensor(rstd[:, h * G:h * G + G], dev[:, h * G:h * G + G], g.neg_half[:, 0:G], ALU.pow)

                pool_l.begin(pool)
                pool.wait_ge(set_up, 3)
                pool.sem_inc(payload_free, 1)
                with pool.Fori(0, B) as it:
                    pool_l.emit(it, {"var": var, "rstd": rstd_})
                    dve_l.wait(pool, it, ("pos_i",))
                    act_l.wait(pool, it, ("second", TB - 1))
                    settle(pool, payload_left)
                    for i in range(2):
                        for t in T:
                            pool.indirect_dma_start(g.xe_dram, bass.IndirectOffsetOnAxis(pos_i[:, i, t:t + 1], 0),
                                                    pay[i][:, t, :], None, bounds_check=X_ROWS - 1).then_inc(scattered, 16)
                    pool.wait_ge(scattered, it * SC + SC)
                    pool.sem_inc(payload_free, 1)
                pool.wait_ge(table_step, 2)
                for e in range(NE):
                    pool.indirect_dma_start(g.xe_dram, bass.IndirectOffsetOnAxis(pos_i[:, 0, e:e + 1], 0),
                                            pay[0][:, e, :], None, bounds_check=X_ROWS - 1).then_inc(pads_in, 16)
                pool.wait_ge(pads_in, 16 * NE)


def tile_table(nc, dve, g, st, pay, pos_i, xt, ready):
    def sb(n, s, d=F32): return st.enter_context(nc.sbuf_tensor(n, s, d))
    step = Ticks(st.enter_context(nc.semaphore("table_ops")))
    T = FFN_TILES
    full = sb("full", [P, NE])
    full_i = sb("full_i", [P, NE], I32)
    tiles = sb("tiles_e", [P, NE])
    cum = sb("cum", [P, NE])
    past = xt[:, :, :].rearrange("p t d -> p (t d)")[:, 0:T * NE].rearrange("p (t e) -> p t e", e=NE)
    expert = sb("expert", [P, T])
    before = sb("before", [P, T])
    row = sb("row", [P, T])
    n = 0

    def then(ins):
        nonlocal n
        n += 1
        ins.then_inc(step.sem, 1)
        step.wait(dve, 0, n)

    def wide(ap, left):
        return (ap.rearrange("p (t o) -> p t o", o=1) if left else ap.rearrange("p (o e) -> p o e", o=1)).to_broadcast([P, T, NE])

    lane = g.step_c[:, g.col["token"].start:g.col["token"].start + 1]
    then(dve.tensor_tensor(full[:, :], g.run[:, :], g.step_c[:, g.col["region"]], ALU.add))
    then(dve.scalar_tensor_tensor(full[:, :], lane.to_broadcast([P, NE]), 0.5, full[:, :], ALU.mult, ALU.add))
    then(dve.tensor_copy(pos_i[:, 0, :], full[:, :]))
    pads = g.col["pads"].start
    dve.tensor_copy(pay[0][:, 0:NE, D].bitcast(I32), g.step_c[:, pads:pads + NE]).then_inc(ready, 1)
    dve.tensor_copy(pay[1][:, 0:SPARE, D].bitcast(I32), g.step_c[:, pads + NE:pads + NE + SPARE]).then_inc(ready, 1)
    then(dve.tensor_scalar(full_i[:, :], g.run[:, :], float(P - 1), None, ALU.add))
    then(dve.tensor_single_scalar(full_i[:, :], full_i[:, :], P.bit_length() - 1, ALU.arith_shift_right))
    then(dve.tensor_copy(tiles[:, :], full_i[:, :]))
    then(dve.tensor_tensor_scan(cum[:, :], g.ones[:, 0:NE], tiles[:, :], 0.0, ALU.mult, ALU.add))
    then(dve.tensor_tensor(past, wide(g.step_c[:, g.col["tiles"]], True), wide(cum[:, :], False), ALU.is_ge))
    then(dve.tensor_reduce(expert[:, :], past, AX.X, ALU.add))
    then(dve.tensor_tensor(past, past, wide(tiles[:, :], False), ALU.mult))
    then(dve.tensor_reduce(before[:, :], past, AX.X, ALU.add))
    then(dve.tensor_tensor(row[:, :], g.step_c[:, g.col["tiles"]], before[:, :], ALU.subtract))
    then(dve.tensor_scalar(row[:, :], row[:, :], float(P), None, ALU.mult))
    then(dve.scalar_tensor_tensor(g.table[:, 0, :], expert[:, :], float(ROWS_E), row[:, :], ALU.mult, ALU.add))
    then(dve.tensor_scalar(g.table[:, 1, :], expert[:, :], float(NE - 1), None, ALU.min))


def experts(nc, g):
    U = 4
    IT = FFN_TILES // U
    HALF = F // 2
    with ExitStack() as st:
        def sb(n, s, d=F32): return st.enter_context(nc.sbuf_tensor(n, s, d))
        def ps(n, s, d=F32): return st.enter_context(nc.psum_tensor(n, s, d))
        def sem(n): return st.enter_context(nc.semaphore(n))

        b2_sb = sb("b2_sb", [P, NE, D])
        xg = [sb(f"xg{i}", [P, PAYLOAD]) for i in range(U)]
        y_row = [sb(f"y_row{i}", [P, 1], I32) for i in range(U)]
        xgT = [sb(f"xgT{i}", [P, KD, P]) for i in range(2)]
        h = sb("h", [P, F])
        hT = [sb(f"hT{i}", [P, FT, P]) for i in range(2)]
        y = [sb(f"y{i}", [P, D]) for i in range(2)]
        pX = [ps(f"pX{i}", [P, KD, P]) for i in range(2)]
        pH = ps("pH", [P, F])
        pHT = ps("pHT", [P, FT, P])
        pY = [ps(f"pY{i}", [P, D]) for i in range(2)]

        R = range(U)
        pe_l = Line(sem("ex_pe"), [x for u in R for x in (("turn_h", u), ("up", u + 1), ("turn_x", u + 2), ("down", u))], credit=False)
        act_l = Line(sem("ex_act"), [x for u in R for x in (("relu", u), ("copy_x", u + 2))], credit=False)
        dve_l = Line(sem("ex_dve"), [x for u in R for x in (("hidden", u + 1), ("keep", u + 2), ("result", u))], credit=False)
        x_in = [Ticks(sem(f"xg_in{i}"), per=1, by=16) for i in R]
        out = [Ticks(sem(f"y_out{i}"), per=1, by=16) for i in R]
        b2_in = sem("b2_in")
        settled_pool, settled_sp = sem("settled_pool"), sem("settled_sp")
        HEAD = {"pe": 3, "act": 2, "dve": 3}

        def wait(eng, line, ahead, it, kind, tile):
            lag = {"up": 1, "turn_x": 2, "copy_x": 2, "hidden": 1, "keep": 2}.get(kind, 0)
            d, u = divmod(tile - lag, U)
            if isinstance(it, int) and it + d < 0:
                v = early[(kind, tile)]
            elif isinstance(it, int) and it + d == IT - 1:
                v = ahead + (IT - 1) * line.per + 1 + sum(
                    exists(IT - 1, n[1]) for n in line.order[:line.index[(kind, u + lag)]])
            else:
                v = (it + d) * line.per + line.index[(kind, u + lag)] + 1 + ahead if isinstance(it, int) else \
                    it * line.per + (d * line.per + line.index[(kind, u + lag)] + 1 + ahead)
            eng.wait_ge(line.sem, v)

        early = {("turn_x", 0): 1, ("turn_x", 1): 2, ("up", 0): 3, ("copy_x", 0): 1, ("copy_x", 1): 2,
                 ("keep", 0): 1, ("keep", 1): 2, ("hidden", 0): 3}
        w_pe = lambda eng, it, kind, tile: wait(eng, pe_l, HEAD["pe"], it, kind, tile)
        w_act = lambda eng, it, kind, tile: wait(eng, act_l, HEAD["act"], it, kind, tile)
        w_dve = lambda eng, it, kind, tile: wait(eng, dve_l, HEAD["dve"], it, kind, tile)

        def exists(it, tile):
            return not isinstance(it, int) or 0 <= it * U + tile < FFN_TILES

        def over(eng, line, ops):
            for it in (0, None, IT - 1):
                if it is None:
                    with eng.Fori(1, IT - 1) as it:
                        line.emit(it, ops)
                else:
                    line.emit(it, ops, skip=lambda name: not exists(it, name[1]))

        def number(eng, it, tile, which):
            top = X_ROWS - P if which == 0 else NE - 1
            return eng.value_load(g.table[0:1, which, bass.ds(it * U + tile, 1)], min_val=0, max_val=top)

        with nc.Block() as block:
            @block.sync
            def _(sp):
                sp.dma_start(b2_sb[:, :, :].rearrange("p e d -> p (e d)"),
                             g.b2.rearrange("(a e) d -> a (e d)", a=1).to_broadcast([P, NE * D])).then_inc(b2_in, 16)

                def load(it, tile):
                    row = number(sp, it, tile, 0)
                    if exists(it, tile - U):
                        w_dve(sp, it, "keep", tile - U)
                        settle(sp, settled_sp)
                        w_pe(sp, it, "turn_x", tile - U)
                        settle(sp, settled_sp)
                    sp.dma_start(xg[tile % U][:, :], g.xe_dram[bass.ds(row, P), :]).then_inc(x_in[tile % U].sem, 16)

                for t in range(3):
                    load(0, t)
                for it in (0, None, IT - 1):
                    if it is None:
                        with sp.Fori(1, IT - 1) as it:
                            for u in R:
                                load(it, u + 3)
                    else:
                        for u in R:
                            if exists(it, u + 3):
                                load(it, u + 3)

            @block.tensor
            def _(pe):
                def turn_x(it, tile):
                    x_in[tile % U].wait(pe, it, tile // U + 1)
                    if exists(it, tile - 2):
                        w_act(pe, it, "copy_x", tile - 2)
                    for k in range(KD):
                        mm = pe.transpose(pX[tile % 2][:, k, :], xg[tile % U][:, k * P:(k + 1) * P], g.ident[:, :])
                    return mm

                def up(it, tile):
                    e = number(pe, it, tile, 1)
                    w_act(pe, it, "copy_x", tile)
                    if exists(it, tile - 1):
                        w_dve(pe, it, "hidden", tile - 1)
                    for half in range(2):
                        for k in range(KD):
                            mm = pe.matmul(pH[:, half * HALF:(half + 1) * HALF], xgT[tile % 2][:, k, :],
                                           g.w1_sb[:, bass.ds(e, 1), k, half * HALF:(half + 1) * HALF]
                                           .rearrange("p e f -> p (e f)"), start=k == 0, stop=k == KD - 1)
                    return mm

                def turn_h(it, tile):
                    w_dve(pe, it, "hidden", tile)
                    if exists(it, tile - 1):
                        w_act(pe, it, "relu", tile - 1)
                    for f in range(FT):
                        mm = pe.transpose(pHT[:, f, :], h[:, f * P:(f + 1) * P], g.ident[:, :])
                    return mm

                def down(it, tile):
                    e = number(pe, it, tile, 1)
                    w_act(pe, it, "relu", tile)
                    if exists(it, tile - 2):
                        w_dve(pe, it, "result", tile - 2)
                    for f in range(FT):
                        mm = pe.matmul(pY[tile % 2][:, :], hT[tile % 2][:, f, :],
                                       g.w2_sb[:, bass.ds(e, 1), f, :].rearrange("p e d -> p (e d)"),
                                       start=f == 0, stop=f == FT - 1)
                    return mm

                g.w1_in.wait(pe, 0, 1)
                g.w2_in.wait(pe, 0, 1)
                turn_x(0, 0).then_inc(pe_l.sem, 1)
                turn_x(0, 1).then_inc(pe_l.sem, 1)
                up(0, 0).then_inc(pe_l.sem, 1)
                over(pe, pe_l, {"turn_x": turn_x, "up": up, "turn_h": turn_h, "down": down})

            @block.scalar
            def _(act):
                def copy_x(it, tile):
                    w_pe(act, it, "turn_x", tile)
                    if exists(it, tile - 2):
                        w_pe(act, it, "up", tile - 2)
                    return act.copy(xgT[tile % 2][:, :, :], pX[tile % 2][:, :, :])

                def relu(it, tile):
                    e = number(act, it, tile, 1)
                    w_pe(act, it, "turn_h", tile)
                    if exists(it, tile - 2):
                        w_pe(act, it, "down", tile - 2)
                    for f in range(FT):
                        ins = act.activation(hT[tile % 2][:, f, :], pHT[:, f, :], ACT.Relu,
                                             bias=g.b1_sb[:, bass.ds(e * FT + f, 1)])
                    return ins

                copy_x(0, 0).then_inc(act_l.sem, 1)
                copy_x(0, 1).then_inc(act_l.sem, 1)
                over(act, act_l, {"copy_x": copy_x, "relu": relu})

            @block.vector
            def _(dve):
                def hidden(it, tile):
                    w_pe(dve, it, "up", tile)
                    if exists(it, tile - 1):
                        w_pe(dve, it, "turn_h", tile - 1)
                    return dve.tensor_copy(h[:, :], pH[:, :])

                def keep(it, tile):
                    x_in[tile % U].wait(dve, it, tile // U + 1)
                    if exists(it, tile - U):
                        out[tile % U].wait(dve, it, tile // U)
                    return dve.tensor_copy(y_row[tile % U][:, :], xg[tile % U][:, D:D + 1].bitcast(I32))

                def result(it, tile):
                    e = number(dve, it, tile, 1)
                    w_pe(dve, it, "down", tile)
                    if exists(it, tile - 2):
                        out[(tile - 2) % U].wait(dve, it, (tile - 2) // U + 1)
                    return dve.tensor_tensor(y[tile % 2][:, :], pY[tile % 2][:, :],
                                             b2_sb[:, bass.ds(e, 1), :].rearrange("p e d -> p (e d)"), ALU.add)

                dve.wait_ge(b2_in, 16)
                keep(0, 0).then_inc(dve_l.sem, 1)
                keep(0, 1).then_inc(dve_l.sem, 1)
                hidden(0, 0).then_inc(dve_l.sem, 1)
                over(dve, dve_l, {"hidden": hidden, "keep": keep, "result": result})

            @block.gpsimd
            def _(pool):
                def scatter(it, tile):
                    w_dve(pool, it, "result", tile)
                    settle(pool, settled_pool)
                    pool.indirect_dma_start(g.ye_dram, bass.IndirectOffsetOnAxis(y_row[tile % U][:, :], 0),
                                            y[tile % 2][:, :], None, bounds_check=Y_ROWS - 1).then_inc(out[tile % U].sem, 16)
                for it in (0, None, IT - 1):
                    if it is None:
                        with pool.Fori(1, IT - 1) as it:
                            for u in R:
                                scatter(it, u)
                    else:
                        for u in R:
                            scatter(it, u)
                for o in out:
                    o.wait(pool, IT - 1, 1)


def combine(nc, g):
    GT, U = 4, 2
    IT = NT // GT // U
    with ExitStack() as st:
        def sb(n, s, d=F32): return st.enter_context(nc.sbuf_tensor(n, s, d))
        def sem(n): return st.enter_context(nc.semaphore(n))

        xr = [sb(f"xr{i}", [P, GT, D]) for i in range(U)]
        yr = [sb(f"yr{i}", [P, GT, 2, D]) for i in range(U)]
        stats = sb("c_stats", [P, GT, 6])
        mv = [sb(f"c_mv{i}", [P, GT, 2]) for i in range(U)]
        dev = [sb(f"c_dev{i}", [P, GT]) for i in range(U)]
        rstd = [sb(f"c_rstd{i}", [P, GT]) for i in range(U)]
        eps = sb("c_eps", [P, GT])

        R, T = range(U), range(GT)
        dve_l = Line(sem("cb_dve"), [x for u in R for x in
                     [("sum", i, u, t) for i in range(2) for t in T] + [("stat", u, t) for t in T]
                     + [("aggr", u, t) for t in T] + ([("norm", u - 1, t) for t in T] if u else [])]
                     + [("norm", U - 1, t) for t in T])
        pool_l = Line(sem("cb_pool"), [(k, u) for u in R for k in ("var", "rstd")])
        loaded = [Ticks(sem(f"cb_in{u}"), per=1, by=32) for u in R]
        stored = [Ticks(sem(f"cb_out{u}"), per=1, by=16, credit=1) for u in R]
        set_up, settled_sp = sem("cb_set_up"), sem("cb_settled_sp")

        def rows(dram, it, u):
            return dram.rearrange("(g t p) d -> p g t d", p=P, t=GT)[:, bass.ds(it * U + u, 1)].rearrange("p g t d -> p (g t) d")

        with nc.Block() as block:
            @block.sync
            def _(sp):
                for s in stored:
                    sp.sem_inc(s.sem, 16)
                y_rows = g.ye_dram[0:2 * B * S, :].rearrange("(n two) d -> n (two d)", two=2)
                with sp.Fori(0, IT) as it:
                    for u in R:
                        stored[u].wait(sp, it, 0)
                        settle(sp, settled_sp)
                        dve_l.wait(sp, it, ("norm", u, GT - 1), ago=1)
                        sp.dma_start(xr[u][:, :, :], rows(g.x2_dram, it, u)).then_inc(loaded[u].sem, 16)
                        sp.dma_start(yr[u][:, :, :, :].rearrange("p t s d -> p t (s d)"), rows(y_rows, it, u)).then_inc(loaded[u].sem, 16)

            @block.scalar
            def _(act):
                with act.Fori(0, IT) as it:
                    for u in R:
                        dve_l.wait(act, it, ("norm", u, GT - 1))
                        act.dma_start(rows(g.out, it, u), xr[u][:, :, :]).then_inc(stored[u].sem, 16)
                for s in stored:
                    s.wait(act, IT - 1, 1)

            @block.vector
            def _(dve):
                def sum_(it, i, u, t):
                    if i == 0 and t == 0:
                        loaded[u].wait(dve, it, 1)
                    if i:
                        dve_l.wait(dve, it, ("sum", 0, u, t))
                    return dve.scalar_tensor_tensor(xr[u][:, t, :], yr[u][:, t, i, :],
                                                    g.c_sum[:, i, bass.ds((it * U + u) * GT + t, 1)], xr[u][:, t, :],
                                                    ALU.mult, ALU.add)

                def stat(it, u, t):
                    dve_l.wait(dve, it, ("sum", 1, u, t))
                    return dve.bn_stats(stats[:, t, :], xr[u][:, t, :])

                def aggr(it, u, t):
                    dve_l.wait(dve, it, ("stat", u, t))
                    if t == 0:
                        dve_l.wait(dve, it, ("norm", u, GT - 1), ago=1)
                        pool_l.wait(dve, it, ("rstd", u), ago=1)
                    settle(dve, g.settled)
                    return dve.bn_aggr(mv[u][:, t, :], stats[:, t, :])

                def norm(it, u, t):
                    pool_l.wait(dve, it, ("rstd", u))
                    return dve.tensor_scalar(xr[u][:, t, :], xr[u][:, t, :], mv[u][:, t, 0:1], rstd[u][:, t:t + 1],
                                             ALU.subtract, ALU.mult)

                dve_l.begin(dve)
                dve.memset(eps[:, :], EPS).then_inc(set_up, 1)
                with dve.Fori(0, IT) as it:
                    dve_l.emit(it, {"sum": sum_, "stat": stat, "aggr": aggr, "norm": norm})

            @block.gpsimd
            def _(pool):
                def var(it, u):
                    dve_l.wait(pool, it, ("aggr", u, GT - 1))
                    return pool.tensor_tensor(dev[u][:, :], mv[u][:, :, 1], eps[:, :], ALU.add)

                def rstd_(it, u):
                    pool_l.wait(pool, it, ("var", u))
                    return pool.tensor_tensor(rstd[u][:, :], dev[u][:, :], g.neg_half[:, 0:GT], ALU.pow)

                pool_l.begin(pool)
                pool.wait_ge(set_up, 1)
                with pool.Fori(0, IT) as it:
                    pool_l.emit(it, {"var": var, "rstd": rstd_})


def kernel(**inputs):
    import concourse.bacc as bacc
    from concourse.bass_utils import run_bass_kernel_spmd

    a = {k: np.asarray(v) for k, v in inputs.items()}
    lay = np.ascontiguousarray
    f32 = np.float32
    p = np.arange(P)[:, None]
    steps = np.concatenate([
        np.broadcast_to(np.arange(NE), (P, NE)),
        np.broadcast_to(np.arange(NE) * ROWS_E, (P, NE)),
        np.broadcast_to(np.arange(FFN_TILES), (P, FFN_TILES)),
        2 * (p + P * np.arange(NT)),
        2 * B * S + p + P * np.arange(NE + SPARE)], axis=1).astype(f32)
    arrays = {
        "x": lay(a["x"].reshape(B * S, D)),
        "xT": lay(a["x"].reshape(B * S, D).T),
        "wqT": lay(a["L0_attn_w_q"].T), "wkT": lay(a["L0_attn_w_k"].T),
        "wvT": lay(a["L0_attn_w_v"].T), "woT": lay(a["L0_attn_w_o"].T),
        "ctxT": lay(a["ctx_1024"].reshape(B * C, D).T),
        "cWqT": lay(a["L0_xattn_Wq"].T), "cbq": lay(a["L0_xattn_bq"].reshape(KD, P).T),
        "cWk": lay(a["L0_xattn_Wk"]), "cbk": lay(a["L0_xattn_bk"].reshape(KD, P).T),
        "cWv": lay(a["L0_xattn_Wv"]), "cbv": lay(a["L0_xattn_bv"]),
        "gate_w": lay(a["L0_ffn_gate_w"]), "gate_b": lay(a["L0_ffn_gate_b"]),
        "w1": lay(a["L0_ffn_w1"]),
        "b1T": lay(a["L0_ffn_b1"].reshape(NE, FT, P).transpose(2, 0, 1).reshape(P, NE * FT)),
        "w2": lay(a["L0_ffn_w2"]), "b2": lay(a["L0_ffn_b2"]),
        "eye": np.eye(P, dtype=f32), "lower": np.triu(np.ones((P, P), f32), 1), "steps": steps,
    }
    nc = bacc.Bacc("TRN2", target_bir_lowering=False, num_devices=1)
    given = {n: nc.dram_tensor(n, v.shape, mybir.dt.from_np(v.dtype), kind="ExternalInput").ap()
             for n, v in arrays.items()}
    out = nc.dram_tensor("out", (B * S, D), F32, kind="ExternalOutput").ap()
    build_program(nc, **given, out=out)
    result = run_bass_kernel_spmd(nc, [arrays], core_ids=[0])
    return result.results[0]["out"].reshape(B, S, D)
```

```python
from contextlib import ExitStack

import numpy as np

import concourse.bass as bass
from concourse import mybir

F32, BF16 = mybir.dt.float32, mybir.dt.bfloat16
I32, U32 = mybir.dt.int32, mybir.dt.uint32
ALU, ACT, AX = mybir.AluOpType, mybir.ActivationFunctionType, mybir.AxisListType

P = 128
B, S, D = 4, 1024, 256
C = 77
CP = 96
H, HD = 16, 16
NE, F = 8, 1024
KD = D // P
TB = S // P
NT = B * TB
FT = F // P
NH = B * H
EPS = 1e-5
BETA = D ** -0.5

Q_PARTS = "hhhmml"
K_PARTS = "hmlhmh"
STACK = 16 * len(Q_PARTS)
FULL = STACK + 3

ROWS_E = B * S + P
FFN_TILES = 2 * NT + NE - 1
SPARE = FFN_TILES - 2 * NT
X_ROWS = NE * ROWS_E + SPARE * P
PAYLOAD = 260
Y_ROWS = 2 * B * S + (NE + SPARE) * P


class Shared:
    pass


class Ticks:

    def __init__(self, sem, per=0, by=1, credit=0):
        self.sem, self.per, self.by, self.credit = sem, per, by, credit

    def value(self, it, k):
        return it * (self.per * self.by) + (k + self.credit) * self.by

    def wait(self, eng, it, k):
        v = self.value(it, k)
        if isinstance(v, int) and v <= 0:
            return
        eng.wait_ge(self.sem, v)


class Line:

    def __init__(self, sem, order, credit=True):
        self.sem, self.order = sem, order
        self.index = {name: i for i, name in enumerate(order)}
        self.per = len(order)
        self.credit = self.per if credit else 0

    def wait(self, eng, it, name, ago=0):
        v = it * self.per + (self.index[name] + 1 + self.credit - ago * self.per)
        if isinstance(v, int) and v <= 0:
            return
        eng.wait_ge(self.sem, v)

    def begin(self, eng):
        if self.credit:
            eng.sem_inc(self.sem, self.credit)

    def emit(self, it, ops, skip=lambda name: False):
        for name in self.order:
            if not skip(name):
                ops[name[0]](it, *name[1:]).then_inc(self.sem, 1)


def settle(eng, sem):
    eng.sem_inc(sem, 1)


def build_program(nc, x, xT, wqT, wkT, wvT, woT, ctxT, cWqT, cbq, cWk, cbk, cWv, cbv,
                  gate_w, gate_b, w1, b1T, w2, b2, eye, lower, steps, out):
    g = Shared()
    g.x, g.xT, g.wqT, g.wkT, g.wvT, g.woT = x, xT, wqT, wkT, wvT, woT
    g.ctxT, g.cWqT, g.cbq, g.cWk, g.cbk, g.cWv = ctxT, cWqT, cbq, cWk, cbk, cWv
    g.cbv, g.gate_w, g.gate_b, g.w1, g.b1T, g.w2 = cbv, gate_w, gate_b, w1, b1T, w2
    g.b2, g.eye, g.lower, g.steps, g.out = b2, eye, lower, steps, out
    g.q_dram = nc.dram_tensor("q_stacks", [NH, STACK, S], BF16).ap()
    g.k_dram = nc.dram_tensor("k_stacks", [NH, STACK, S], BF16).ap()
    g.xe_dram = nc.dram_tensor("x_by_expert", [X_ROWS, PAYLOAD], F32).ap()
    g.ye_dram = nc.dram_tensor("y_by_token", [Y_ROWS, D], F32).ap()
    g.x2_dram = nc.dram_tensor("x2", [B * S, D], F32).ap()

    with ExitStack() as st:
        def sb(n, s, d=F32): return st.enter_context(nc.sbuf_tensor(n, s, d))
        def sem(n, **kw): return Ticks(st.enter_context(nc.semaphore(n)), **kw)

        g.ident = sb("ident", [P, P])
        g.ident_b = sb("ident_b", [P, P], BF16)
        g.below = sb("below", [P, P])
        g.ones = sb("ones", [P, P])
        g.step_c = sb("step_c", [P, steps.shape[1]])
        g.c_sum = sb("c_weights", [P, 2, NT])
        g.run = sb("run", [P, NE])
        g.gate_sb = sb("gate_w_sb", [P, KD, NE])
        g.gate_b_sb = sb("gate_b_sb", [P, NE])
        g.woT_sb = sb("woT_sb", [P, KD, D])
        g.b1_sb = sb("b1T_sb", [P, NE * FT])
        g.fold = sb("fold", [P, KD, B * C])
        g.fold_b = sb("fold_b", [1, B * C])
        g.cv = sb("cv", [CP, B, D])
        g.neg_half = sb("neg_half", [P, TB])
        g.w1_sb = sb("w1_sb", [P, NE, KD, F])
        g.table = sb("table", [P, 2, FFN_TILES], I32)
        g.attn = sb("attn", [P, NH, TB, HD])

        g.x2_tiles = g.attn[:, :, :, :].rearrange("p h t d -> p (h t d)").rearrange("p (t d) -> p t d", d=D)

        g.x2_in = sem("x2_in", by=16)
        g.w1_in = sem("w1_in", by=16)
        g.w2_in = sem("w2_in", by=16)
        g.const_in = sem("const_in", by=16)
        g.made = sem("constants_made")
        g.settled = sem("settled").sem
        g.col = {}
        at = 0
        for name, n in (("iota8", NE), ("region", NE), ("tiles", FFN_TILES), ("token", NT),
                        ("pads", NE + SPARE), ("anew", NE * (TB + 1))):
            g.col[name] = slice(at, at + n)
            at += n

        with nc.sbuf_tensor("v_all", [P, NH, TB, HD], F32) as g.v_all:
            project(nc, g)
            attend(nc, g)
        with nc.sbuf_tensor("w2_sb", [P, NE, FT, D], F32) as g.w2_sb:
            norm_route(nc, g)
            experts(nc, g)
        combine(nc, g)


def project(nc, g):
    with ExitStack() as st:
        def sb(n, s, d=F32): return st.enter_context(nc.sbuf_tensor(n, s, d))
        def ps(n, s, d=F32): return st.enter_context(nc.psum_tensor(n, s, d))
        def sem(n, **kw): return Ticks(st.enter_context(nc.semaphore(n)), **kw)

        CH = 512
        NC = S // CH
        U = 2
        w_qk = sb("w_qk", [P, 2, KD, D])
        w_v = sb("w_v", [P, KD, D])
        xs = sb("xs", [P, U, KD, S])
        part = sb("part", [P, 4, 3, S], BF16)
        rest = sb("rest", [P, 4, CH])
        c_x = sb("c_x", [P, KD, B * C])
        c_w = sb("c_w", [P, 3, KD, D])
        c_bk = sb("c_bk", [P, KD])
        c_bq = sb("c_bq", [P, KD])
        c_bv = sb("c_bv", [1, D])
        c_k = sb("c_k", [P, KD, B * C])
        pq = [ps(f"pq{i}", [P, CH]) for i in range(4)]
        pv = [ps(f"pv{i}", [P, CH]) for i in range(2)]
        pc = [ps(f"pc{i}", [P, CH]) for i in range(2)]

        qk_in = sem("qk_in", by=16)
        v_in = sem("v_in", by=16)
        cross_in = sem("cross_in", by=16)
        x_in = [sem(f"x_in{u}", per=1, by=16 * KD) for u in range(U)]
        NQ = 4 * NC
        NV = TB // 2
        qk_done = sem("qk_done", per=U * NQ, credit=U * NQ)
        v_done = sem("v_done", per=U * NV, credit=U * NV)
        h_done = sem("h_done", per=U * NQ, credit=U * NQ)
        rest_done = sem("rest_done", per=U * NQ, credit=U * NQ)
        m_done = sem("m_done", per=U * NQ, credit=U * NQ)
        l_done = sem("l_done", per=U * NQ, credit=U * NQ)
        v_out = sem("v_out", per=U * NV, credit=U * NV)
        stored = [sem(f"stored{i}", per=U, by=16 * len(Q_PARTS), credit=U) for i in range(4)]
        cross_mm = sem("cross_mm")
        cross_k = sem("cross_k")
        cross_out = sem("cross_out")
        cv_zero = sem("cv_zero")

        with nc.Block() as block:
            @block.sync
            def _(sp):
                sp.dma_start(w_qk[:, 0], g.wqT.rearrange("(k p) n -> p k n", p=P)).then_inc(qk_in.sem, 16)
                sp.dma_start(w_qk[:, 1], g.wkT.rearrange("(k p) n -> p k n", p=P)).then_inc(qk_in.sem, 16)
                sp.dma_start(w_v[:, :, :], g.wvT.rearrange("(k p) n -> p k n", p=P)).then_inc(v_in.sem, 16)
                for i in range(4):
                    sp.sem_inc(stored[i].sem, stored[i].value(0, 0))
                with sp.Fori(0, B // U) as it:
                    for u in range(U):
                        for j in range(4):
                            which, m = divmod(j, KD)
                            l_done.wait(sp, it, u * NQ + NC * (j + 1))
                            order, dst = ((Q_PARTS, g.q_dram), (K_PARTS, g.k_dram))[which]
                            head = (it * U + u) * H + m * (H // KD)
                            for r, name in enumerate(order):
                                sp.dma_start(dst[bass.ds(head, H // KD), 16 * r:16 * r + 16, :],
                                             part[:, j, "hml".index(name), :]).then_inc(stored[j].sem, 16)
                for i in range(4):
                    stored[i].wait(sp, B // U - 1, U)

            @block.scalar
            def _(act):
                act.dma_start(g.ident[:, :], g.eye).then_inc(g.const_in.sem, 16)
                act.dma_start(g.below[:, :], g.lower).then_inc(g.const_in.sem, 16)
                act.dma_start(g.step_c[:, :], g.steps).then_inc(g.const_in.sem, 16)
                act.dma_start(g.gate_sb[:, :, :], g.gate_w.rearrange("(k p) n -> p k n", p=P)).then_inc(g.const_in.sem, 16)
                act.dma_start(g.gate_b_sb[:, :], g.gate_b.rearrange("(a n) -> a n", a=1).to_broadcast([P, NE])).then_inc(g.const_in.sem, 16)
                act.dma_start(g.woT_sb[:, :, :], g.woT.rearrange("(k p) n -> p k n", p=P)).then_inc(g.const_in.sem, 16)
                act.dma_start(g.b1_sb[:, :], g.b1T).then_inc(g.const_in.sem, 16)
                act.dma_start(c_x[:, :, :], g.ctxT.rearrange("(k p) n -> p k n", p=P)).then_inc(cross_in.sem, 16)
                for i, w in enumerate((g.cWk, g.cWqT, g.cWv)):
                    act.dma_start(c_w[:, i], w.rearrange("(k p) n -> p k n", p=P)).then_inc(cross_in.sem, 16)
                act.dma_start(c_bk[:, :], g.cbk).then_inc(cross_in.sem, 16)
                act.dma_start(c_bq[:, :], g.cbq).then_inc(cross_in.sem, 16)
                act.dma_start(c_bv[:, :], g.cbv.rearrange("(a n) -> a n", a=1)).then_inc(cross_in.sem, 16)
                act.sem_inc(h_done.sem, U * NQ)
                act.sem_inc(m_done.sem, U * NQ)
                act.sem_inc(v_out.sem, U * NV)
                with act.Fori(0, B // U) as it:
                    def parts_h(i):
                        u, j, c = i // NQ, i // NC % 4, i % NC
                        qk_done.wait(act, it, i + 1)
                        stored[j].wait(act, it, u)
                        act.copy(part[:, j, 0, c * CH:(c + 1) * CH], pq[i % 4][:, :]).then_inc(h_done.sem, 1)

                    def parts_m(i):
                        j, c = i // NC % 4, i % NC
                        rest_done.wait(act, it, i + 1)
                        act.copy(part[:, j, 1, c * CH:(c + 1) * CH], rest[:, i % 4, :]).then_inc(m_done.sem, 1)

                    def take_v(n):
                        u, pair = divmod(n, NV)
                        v_done.wait(act, it, n + 1)
                        tile = pv[n % 2][:, :].rearrange("p (t h d) -> p t h d", t=2, h=H)
                        for t in range(2):
                            ins = act.copy(g.v_all[:, bass.ds((it * U + u) * H, H), 2 * pair + t, :], tile[:, t])
                        ins.then_inc(v_out.sem, 1)

                    for u in range(U):
                        for i in range(u * NQ, (u + 1) * NQ):
                            parts_h(i)
                            if i:
                                parts_m(i - 1)
                        for n in range(u * NV, (u + 1) * NV):
                            take_v(n)
                    parts_m(U * NQ - 1)
                for m in range(KD):
                    cross_mm.wait(act, 0, m + 1)
                    cross_in.wait(act, 0, 7)
                    act.activation(c_k[:, m, :], pc[m][:, 0:B * C], ACT.Identity, bias=c_bk[:, m:m + 1]
                                   ).then_inc(cross_k.sem, 1)

            @block.vector
            def _(dve):
                dve.sem_inc(rest_done.sem, U * NQ)
                dve.sem_inc(l_done.sem, U * NQ)
                dve.memset(g.ones[:, :], 1.0).then_inc(g.made.sem, 1)
                dve.memset(g.run[:, :], 0.0).then_inc(g.made.sem, 1)
                dve.memset(g.cv[64:CP, :, :], 0.0).then_inc(cv_zero.sem, 1)
                dve.memset(g.neg_half[:, :], -0.5).then_inc(g.made.sem, 1)
                g.const_in.wait(dve, 0, 7)
                dve.tensor_copy(g.ident_b[:, :], g.ident[:, :]).then_inc(g.made.sem, 1)
                with dve.Fori(0, B // U) as it:
                    def parts_l(i):
                        at = i // NC % 4, slice(i % NC * CH, (i % NC + 1) * CH)
                        m_done.wait(dve, it, i + 1)
                        dve.tensor_tensor(part[:, at[0], 2, at[1]], rest[:, i % 4, :], part[:, at[0], 1, at[1]],
                                          ALU.subtract).then_inc(l_done.sem, 1)

                    for i in range(U * NQ):
                        at = i // NC % 4, slice(i % NC * CH, (i % NC + 1) * CH)
                        h_done.wait(dve, it, i + 1)
                        l_done.wait(dve, it, i - 3)
                        dve.tensor_tensor(rest[:, i % 4, :], pq[i % 4][:, :], part[:, at[0], 0, at[1]],
                                          ALU.subtract).then_inc(rest_done.sem, 1)
                        if i:
                            parts_l(i - 1)
                    parts_l(U * NQ - 1)
                for m in range(KD):
                    cross_mm.wait(dve, 0, KD + 1 + m)
                    dve.tensor_scalar(g.fold[:, m, :], pc[m][:, 0:B * C], BETA, None, ALU.mult).then_inc(cross_out.sem, 1)
                cross_mm.wait(dve, 0, 2 * KD + 1)
                dve.tensor_scalar(g.fold_b[:, :], pv[0][0:1, 0:B * C], BETA, None, ALU.mult).then_inc(cross_out.sem, 1)
                cv_zero.wait(dve, 0, 1)
                for b in range(B):
                    cross_mm.wait(dve, 0, 2 * KD + 2 + b)
                    dve.tensor_copy(g.cv[0:C, b, :], pq[b][0:C, 0:D]).then_inc(cross_out.sem, 1)

            @block.gpsimd
            def _(pool):
                with pool.Fori(0, B // U) as it:
                    for u in range(U):
                        qk_done.wait(pool, it, (u + 1) * NQ - U * NQ)
                        v_done.wait(pool, it, (u + 1) * NV - U * NV)
                        for k in range(KD):
                            pool.dma_start(xs[:, u, k, :], g.xT[k * P:(k + 1) * P, bass.ds((it * U + u) * S, S)]
                                           ).then_inc(x_in[u].sem, 16)

            @block.tensor
            def _(pe):
                pe.sem_inc(qk_done.sem, U * NQ)
                pe.sem_inc(v_done.sem, U * NV)
                qk_in.wait(pe, 0, 2)
                v_in.wait(pe, 0, 1)
                with pe.Fori(0, B // U) as it:
                    for u in range(U):
                        x_in[u].wait(pe, it, 1)
                        for i in range(u * NQ, (u + 1) * NQ):
                            w, m, c = i // NC // KD % 2, i // NC % KD, i % NC
                            rest_done.wait(pe, it, i - 3)
                            for k in range(KD):
                                mm = pe.matmul(pq[i % 4][:, :], w_qk[:, w, k, m * P:(m + 1) * P],
                                               xs[:, u, k, c * CH:(c + 1) * CH], start=k == 0, stop=k == KD - 1)
                            mm.then_inc(qk_done.sem, 1)
                        for n in range(u * NV, (u + 1) * NV):
                            v_out.wait(pe, it, n - 1)
                            for t in range(2):
                                tok = (2 * (n % NV) + t) * P
                                for k in range(KD):
                                    mm = pe.matmul(pv[n % 2][:, t * D:(t + 1) * D], xs[:, u, k, tok:tok + P],
                                                   w_v[:, k, :], start=k == 0, stop=k == KD - 1)
                            mm.then_inc(v_done.sem, 1)
                cross_in.wait(pe, 0, 7)
                for m in range(KD):
                    for k in range(KD):
                        mm = pe.matmul(pc[m][:, 0:B * C], c_w[:, 0, k, m * P:(m + 1) * P], c_x[:, k, :],
                                       start=k == 0, stop=k == KD - 1)
                    mm.then_inc(cross_mm.sem, 1)
                for m in range(KD):
                    cross_k.wait(pe, 0, KD)
                    for k in range(KD):
                        mm = pe.matmul(pc[m][:, 0:B * C], c_w[:, 1, k, m * P:(m + 1) * P], c_k[:, k, :],
                                       start=k == 0, stop=k == KD - 1)
                    mm.then_inc(cross_mm.sem, 1)
                v_out.wait(pe, B // U - 1, U * NV)
                for k in range(KD):
                    mm = pe.matmul(pv[0][0:1, 0:B * C], c_bq[:, k:k + 1], c_k[:, k, :],
                                   start=k == 0, stop=k == KD - 1)
                mm.then_inc(cross_mm.sem, 1)
                rest_done.wait(pe, B // U - 1, U * NQ)
                g.made.wait(pe, 0, 4)
                for b in range(B):
                    for k in range(KD):
                        pe.matmul(pq[b][0:C, 0:D], c_x[:, k, b * C:(b + 1) * C], c_w[:, 2, k, :],
                                  start=k == 0, stop=False)
                    pe.matmul(pq[b][0:C, 0:D], g.ones[0:1, 0:C], c_bv[:, :],
                              start=False, stop=True).then_inc(cross_mm.sem, 1)


def attend(nc, g):
    LEAD = 15
    U = 4
    UN = U * TB
    IT = NH // U
    HALF = S // 2
    SCALE = float(HD) ** -0.5
    VW = 32
    W1_PIECES = NE * KD // IT
    g.w1_loads = IT
    with ExitStack() as st:
        def sb(n, s, d=F32): return st.enter_context(nc.sbuf_tensor(n, s, d))
        def ps(n, s, d=F32): return st.enter_context(nc.psum_tensor(n, s, d))
        def sem(n, **kw): return Ticks(st.enter_context(nc.semaphore(n)), **kw)

        qs = [sb(f"qs{i}", [FULL, S], BF16) for i in range(U)]
        ks = [sb(f"ks{i}", [FULL, S], BF16) for i in range(U)]
        vs = [sb(f"vs{i}", [P, TB, VW]) for i in range(2)]
        ex = [sb(f"ex{i}", [P, S]) for i in range(4)]
        o_sb = [sb(f"o_sb{i}", [P, D]) for i in range(2)]
        mx = [sb(f"mx{i}", [P, TB]) for i in range(2)]
        neg = sb("neg", [P, TB])
        left = sb("left", [P, TB])
        minus = sb("minus", [P, TB])
        neg_parts = [sb(f"neg_parts{i}", [P, 3, TB], BF16) for i in range(2)]
        neg_rows = [sb(f"neg_rows{i}", [3 * TB, P], BF16) for i in range(2)]
        rec = [sb(f"rec{i}", [P, TB]) for i in range(2)]
        pa = [ps(f"pa{i}", [P, S]) for i in range(2)]
        pb = [ps(f"pb{i}", [P, HALF]) for i in range(2)]
        po = [ps(f"po{i}", [P, HALF]) for i in range(2)]

        loaded = [sem(f"loaded{i}", per=1, by=32) for i in range(U)]
        rows_in = [sem(f"rows_in{i}", per=1, by=16) for i in range(U)]
        a_done = sem("a_done", per=UN)
        max_done = sem("max_done", per=UN)
        POOL_OPS = 6
        pool_step = sem("pool_step", per=POOL_OPS * U)
        parts_t = sem("parts_t", per=U)
        parts_out = sem("parts_out", per=U)
        b_done = sem("b_done", per=2 * UN)
        e_done = sem("e_done", per=2 * UN)
        pv_done = sem("pv_done", per=UN)
        o_out = sem("o_out", per=U)
        o_t = sem("o_t", per=U)
        rec_done = sem("rec_done", per=U)
        norm_done = sem("norm_done", per=U)
        set_up = sem("set_up")

        def over(eng, body):
            body(0)
            with eng.Fori(1, IT - 1) as it:
                body(it)
            body(IT - 1)

        def there(it, i):
            return not isinstance(it, int) or 0 <= it * U + i < NH

        with nc.Block() as block:
            @block.sync
            def _(sp):
                def load(it, i):
                    b_done.wait(sp, it, 2 * TB * (i - U + 1))
                    head = it * U + i
                    sp.dma_start(qs[i % U][0:STACK, :], g.q_dram[bass.ds(head, 1)].rearrange("h r t -> (h r) t")
                                 ).then_inc(loaded[i % U].sem, 16)
                    sp.dma_start(ks[i % U][0:STACK, :], g.k_dram[bass.ds(head, 1)].rearrange("h r t -> (h r) t")
                                 ).then_inc(loaded[i % U].sem, 16)

                def rows(it, i):
                    parts_out.wait(sp, it, i + 1)
                    sp.dma_start(qs[i % U][STACK:FULL, :], neg_rows[i % 2][:, :]).then_inc(rows_in[i % U].sem, 16)

                for i in range(3):
                    load(0, i)
                rows(0, 0)

                def body(it):
                    for i in range(U):
                        if there(it, i + 3):
                            load(it, i + 3)
                        if there(it, i + 1):
                            rows(it, i + 1)
                    sp.dma_start(g.w1_sb[:, :, :, :].rearrange("p e k f -> p (e k) f")[:, bass.ds(it * W1_PIECES, W1_PIECES)],
                                 g.w1.rearrange("e (k p) f -> p (e k) f", p=P)[:, bass.ds(it * W1_PIECES, W1_PIECES)]
                                 ).then_inc(g.w1_in.sem, 16)
                over(sp, body)

            @block.gpsimd
            def _(pool):
                one = g.ones[:, :]
                set_up.wait(pool, 0, U + 3)
                g.made.wait(pool, 0, 4)

                def chain(it, i, j, op):
                    pool_step.wait(pool, it, POOL_OPS * i + j)
                    op().then_inc(pool_step.sem, 1)

                def values(it, i):
                    pv_done.wait(pool, it, TB * (i - 1))
                    chain(it, i, 0, lambda: pool.tensor_tensor(
                        vs[i % 2][:, :, 0:HD], g.v_all[:, bass.ds(it * U + i, 1)].rearrange("p h t d -> p (h t) d"),
                        one.rearrange("p (t d) -> p t d", t=TB), ALU.mult))

                def split(it, i):
                    max_done.wait(pool, it, TB * (i + 1))
                    parts_t.wait(pool, it, i - 1)
                    dst, src = neg_parts[i % 2], mx[i % 2][:, :]
                    chain(it, i, 1, lambda: pool.tensor_tensor(neg[:, :], src, minus[:, :], ALU.mult))
                    chain(it, i, 2, lambda: pool.tensor_tensor(dst[:, 0, :], neg[:, :], one[:, 0:TB], ALU.mult))
                    chain(it, i, 3, lambda: pool.tensor_tensor(left[:, :], neg[:, :], dst[:, 0, :], ALU.subtract))
                    chain(it, i, 4, lambda: pool.tensor_tensor(dst[:, 1, :], left[:, :], one[:, 0:TB], ALU.mult))
                    chain(it, i, 5, lambda: pool.tensor_tensor(dst[:, 2, :], left[:, :], dst[:, 1, :], ALU.subtract))

                values(0, 0)
                split(0, 0)

                def body(it):
                    for i in range(U):
                        if there(it, i + 1):
                            values(it, i + 1)
                            split(it, i + 1)
                over(pool, body)

            @block.tensor
            def _(pe):
                def score_max(it, n):
                    i, t = divmod(n, TB)
                    if t == 0:
                        loaded[i % U].wait(pe, it, i // U + 1)
                    max_done.wait(pe, it, n - 1)
                    for half in range(2):
                        mm = pe.matmul(pa[n % 2][:, half * HALF:(half + 1) * HALF],
                                       qs[i % U][0:STACK, t * P:(t + 1) * P],
                                       ks[i % U][0:STACK, half * HALF:(half + 1) * HALF], start=True, stop=True)
                    mm.then_inc(a_done.sem, 1)

                def score_exp(it, n):
                    i, t = divmod(n, TB)
                    if t == 0:
                        rows_in[i % U].wait(pe, it, i // U + 1)
                    for half in range(2):
                        e_done.wait(pe, it, 2 * n - 1 + half)
                        pe.matmul(pb[half][:, :], ks[i % U][:, t * P:(t + 1) * P],
                                  qs[i % U][:, half * HALF:(half + 1) * HALF], start=True, stop=True
                                  ).then_inc(b_done.sem, 1)

                def values(it, n):
                    i, t = divmod(n, TB)
                    if t == 0:
                        pool_step.wait(pe, it, POOL_OPS * i + 1)
                        norm_done.wait(pe, it, i - 1)
                        parts_out.wait(pe, it, i + 1)
                    e_done.wait(pe, it, 2 * n + 2)
                    for j in range(4):
                        mm = pe.matmul(po[i % 2][32 * j:32 * j + VW, 0:D], vs[i % 2][:, t, :],
                                       ex[n % 4][:, j * D:(j + 1) * D], start=t == 0, stop=t == TB - 1,
                                       tile_position=(0, 32 * j))
                    mm.then_inc(pv_done.sem, 1)

                def turn_output(it, i):
                    o_out.wait(pe, it, i + 1)
                    for t in range(2):
                        mm = pe.transpose(po[i % 2][:, D + t * P:D + (t + 1) * P], o_sb[i % 2][:, t * P:(t + 1) * P],
                                          g.ident[:, :])
                    mm.then_inc(o_t.sem, 1)

                def turn_parts(it, i):
                    pool_step.wait(pe, it, POOL_OPS * (i + 1))
                    norm_done.wait(pe, it, i - 1)
                    pe.transpose(po[i % 2][0:3 * TB, 0:P // 2].bitcast(BF16),
                                 neg_parts[i % 2][:, :, :].rearrange("p a t -> p (a t)"), g.ident_b[:, :]
                                 ).then_inc(parts_t.sem, 1)

                g.const_in.wait(pe, 0, 7)
                g.made.wait(pe, 0, 4)
                set_up.wait(pe, 0, U + 2)
                for n in range(TB):
                    score_max(0, n)
                turn_parts(0, 0)
                for n in range(TB, LEAD):
                    score_max(0, n)
                score_exp(0, 0)

                def body(it):
                    for n in range(UN):
                        i, t = divmod(n, TB)
                        if t == 2 and there(it, i - 1):
                            turn_output(it, i - 1)
                        if t == 5 and there(it, i + 1):
                            turn_parts(it, i + 1)
                        if there(it, (n + 1) // TB):
                            score_exp(it, n + 1)
                        values(it, n)
                        if there(it, (n + LEAD) // TB):
                            score_max(it, n + LEAD)
                over(pe, body)
                turn_output(IT, -1)

            @block.scalar
            def _(act):
                def exponentials(it, n):
                    for half in range(2):
                        b_done.wait(act, it, 2 * n + 1 + half)
                        if half == 0:
                            pv_done.wait(act, it, n - 3)
                        act.activation(ex[n % 4][:, half * HALF:(half + 1) * HALF], pb[half][:, :], ACT.Exp,
                                       scale=SCALE).then_inc(e_done.sem, 1)

                def take_output(it, i):
                    pv_done.wait(act, it, TB * (i + 1))
                    o_t.wait(act, it, i - 1)
                    act.copy(o_sb[i % 2][:, :], po[i % 2][:, 0:D]).then_inc(o_out.sem, 1)

                def take_parts(it, i):
                    parts_t.wait(act, it, i + 1)
                    rows_in[(i - 2) % U].wait(act, it, (i - 2) // U + 1)
                    act.copy(neg_rows[i % 2][:, :], po[i % 2][0:3 * TB, 0:P // 2].bitcast(BF16)).then_inc(parts_out.sem, 1)

                take_parts(0, 0)

                def body(it):
                    for n in range(UN):
                        i, t = divmod(n, TB)
                        exponentials(it, n)
                        if t == 0 and there(it, i - 1):
                            take_output(it, i - 1)
                        if t == 5 and there(it, i + 1):
                            take_parts(it, i + 1)
                over(act, body)
                take_output(IT, -1)

            @block.vector
            def _(dve):
                def maxima(it, n):
                    i, t = divmod(n, TB)
                    if t == 0:
                        pool_step.wait(dve, it, POOL_OPS * (i - 1))
                    a_done.wait(dve, it, n + 1)
                    dve.tensor_reduce(mx[i % 2][:, t:t + 1], pa[n % 2][:, :], AX.X, ALU.max).then_inc(max_done.sem, 1)

                def normalise(it, i):
                    o_t.wait(dve, it, i + 1)
                    tile = po[i % 2][:, D:2 * D].rearrange("p (t j d) -> p t j d", t=2, j=4)
                    r = rec[i % 2][:, :].rearrange("p (j t) -> p t j", j=4)
                    dve.reciprocal(r, tile[:, :, :, HD]).then_inc(rec_done.sem, 1)
                    rec_done.wait(dve, it, i + 1)
                    dst = g.attn[:, bass.ds(it * U + i, 1)].rearrange("p h (j t) d -> p t (h j) d", j=4)
                    dve.tensor_tensor(dst, tile[:, :, :, 0:HD],
                                      r.rearrange("p t (j o) -> p t j o", o=1).to_broadcast([P, 2, 4, HD]),
                                      ALU.mult).then_inc(norm_done.sem, 1)

                for i in range(U):
                    dve.memset(ks[i][STACK:FULL, :], 1.0).then_inc(set_up.sem, 1)
                for i in range(2):
                    dve.memset(vs[i][:, :, HD:VW], 1.0).then_inc(set_up.sem, 1)
                dve.memset(minus[:, :], -1.0).then_inc(set_up.sem, 1)
                for n in range(LEAD):
                    maxima(0, n)

                def body(it):
                    for n in range(UN):
                        i, t = divmod(n, TB)
                        if there(it, (n + LEAD) // TB):
                            maxima(it, n + LEAD)
                        if t == 2 and there(it, i - 1):
                            normalise(it, i - 1)
                over(dve, body)
                normalise(IT, -1)


def norm_route(nc, g):
    G = TB // 2
    LAG = {"A": 0, "A'": 1, "B": 1, "B'": 2, "C": 2, "F": 2}
    with ExitStack() as st:
        def sb(n, s, d=F32): return st.enter_context(nc.sbuf_tensor(n, s, d))
        def ps(n, s, d=F32): return st.enter_context(nc.psum_tensor(n, s, d))
        def sem(n): return st.enter_context(nc.semaphore(n))

        x1 = sb("x1", [P, TB, D])
        x_sb = g.w2_sb[:, NE - 1]
        x2 = sb("x2_sb", [P, TB, D])
        room = g.attn[:, :, :, :].rearrange("p h t d -> p (h t d)")
        pad_rows = room[:, TB * PAYLOAD:(TB + NE + SPARE) * PAYLOAD].rearrange("p (e w) -> p e w", w=PAYLOAD)
        pay = [room[:, 0:TB * PAYLOAD].rearrange("p (t w) -> p t w", w=PAYLOAD), sb("pay1", [P, TB, PAYLOAD])]
        at = sb("at", [P, D])
        turned = {ph: sb(f"turned_{ph}", [P, KD, P]) for ph in "ABC"}
        pr = sb("pr", [P, CP])
        prT = sb("prT", [CP, P])
        stats = {ph: sb(f"stats_{ph}", [P, TB, 6]) for ph in "AB"}
        mv = {ph: sb(f"mv_{ph}", [P, TB, 2]) for ph in "AB"}
        dev = {ph: sb(f"dev_{ph}", [P, TB]) for ph in "AB"}
        rstd = {ph: sb(f"rstd_{ph}", [P, TB]) for ph in "AB"}
        eps = sb("eps", [P, TB])
        cneg = sb("cneg", [P, TB])
        csum = sb("csum", [P, TB])
        crec = sb("crec", [P, TB])
        lg = sb("lg", [P, TB, NE])
        top = sb("top", [P, TB, 8])
        top_i = sb("top_i", [P, TB, 8], U32)
        top_f = sb("top_f", [P, TB, 2])
        hot = [sb(f"hot{i}", [P, TB, NE]) for i in range(2)]
        both = sb("both", [P, TB, NE])
        gap = sb("gap", [P, TB])
        gap_e = sb("gap_e", [P, TB])
        count = sb("count", [P, NE, TB + 1])
        base = sb("base", [P, NE, TB + 1])
        pos = sb("pos", [P, TB, NE])
        picked = sb("picked", [P, TB, NE])
        pos_f = sb("pos_f", [P, 2, TB])
        pos_i = sb("pos_i", [P, 2, TB], I32)
        pad_i = sb("pad_i", [P, NE], I32)
        pT = {ph: ps(f"pT_{ph}", [P, KD, P]) for ph in "ABC"}
        pO = {ph: ps(f"pO_{ph}", [P, D]) for ph in "AB"}
        pS = ps("pS", [P, 512])
        pPT = ps("pPT", [CP, P])
        pG = ps("pG", [P, 3, TB, NE])

        T = range(TB)

        def timeline(per_tile, single):
            events = [(tick, (ph, (kind, tick - lag))) for tick in range(2 * TB) for ph, kind, lag in per_tile
                      if tick - lag in T]
            events += [(tick + 0.5, (ph, name)) for ph, name, tick in single]
            return [e for _, e in sorted(events, key=lambda e: e[0])]

        FILLER = ((6, 2, 0), (2, 1, 8))
        pe_t = timeline([("B", "score", 1), ("B", "turn_1", 0), ("C", "gate", 1), ("C", "turn_2", 0),
                         ("B", "cross", 3), ("B", "turn_p", 2), ("A", "proj", 3), ("A", "turn_a", 2)],
                        [("C", ("rank",), 10), ("C", ("total",), 10)]
                        + [("keep_warm", (n, ago), tick) for n, ago, tick in FILLER])
        act_t = timeline([("B", "copy_1", 0), ("C", "copy_2", 0), ("B", "soft", 1), ("F", "fill_0", 2), ("F", "fill_1", 2),
                          ("B", "copy_p", 2), ("A", "copy_a", 2), ("A", "gather", 1)],
                         [("C", ("gap_exp",), 11)])
        act_last = [e for e in act_t if e[0] == "C" and e[1][0] == "copy_2"]
        act_last += [e for e in act_t if e[0] == "F"] + [("C", ("gap_exp",))]
        dve_t = timeline([("B", "rec", 2), ("B", "max", 1), ("A", "stat_1", 4), ("B", "mix", 3), ("A", "aggr_1", 4), ("B", "aggr_2", 4),
                          ("A", "add", 3), ("B", "stat_2", 3)],
                         [("B", ("norm_2", t), 8) for t in T[:G]] + [("A", ("norm_1", t), 8) for t in T[:G]]
                         + [("B'", ("norm_2", t), (t - G) // 2) for t in T[G:]] + [("A'", ("norm_1", t), (t - G) // 2) for t in T[G:]]
                         + [("C", ("logits",), 8)]
                         + [("C", ("top", t), 8) for t in T] + [("C", ("top_i", t), 9) for t in T]
                         + [("C", (k,), 9) for k in ("top_f", "hot_0", "hot_1", "both", "gap")]
                         + [("C", (k,), 10) for k in ("count_0", "count", "base", "run", "pos", "region")]
                         + [("C", (k,), 11) for k in ("pick_0", "sum_0", "pick_1", "sum_1", "row_0", "row_1", "pos_i",
                                                      "one_plus", "w_first", "w_second")])
        pool_t = [(ph, (k, h)) for h in range(2) for ph in "BA" for k in ("var", "rstd")]

        def lines(engine, events):
            return {ph: Line(sem(f"{engine}_{ph}".replace("'", "_late")), [name for p, name in events if p == ph])
                    for ph in sorted({p for p, _ in events}) if ph in LAG}

        pe_l, act_l, dve_l, pool_l = (lines(n, t) for n, t in
                                      (("pe", pe_t), ("act", act_t), ("dve", dve_t), ("pool", pool_t)))

        def start(own):
            def give(eng):
                for line in own.values():
                    line.begin(eng)
            return give

        def body(it, own, events, ops):
            for ph, name in events:
                if ph == "keep_warm":
                    ops[ph](it, *name)
                    continue
                if not isinstance(it, int) or 0 <= it - LAG[ph] < B:
                    ops[name[0]](it, *name[1:]).then_inc(own[ph].sem, 1)

        def over(eng, step, between=None):
            step(0)
            step(1)
            with eng.Fori(2, B) as it:
                step(it)
            if between:
                between()
            step(B)
            step(B + 1)

        def before(kind, t, ago):
            return {"name": (kind, t - 1), "ago": ago} if t else {"name": (kind, TB - 1), "ago": ago + 1}

        def half(t, ph, ago):
            return (ph if t < G else ph + "'"), {"name": (f"norm_{1 + LAG[ph]}", t), "ago": ago}

        x_in = sem("nr_x_in")
        scattered = [sem(f"scattered{t}") for t in T]
        x2_out = [sem(f"x2_out{h}") for h in range(2)]
        payload_left = sem("payload_left")
        set_up, pads_ready, pads_at, pads_in, spare_in = (
            sem(n) for n in ("nr_set_up", "pads_ready", "pads_at", "pads_in", "spare_in"))

        with nc.Block() as block:
            @block.sync
            def _(sp):
                def load_w2(e):
                    sp.dma_start(g.w2_sb[:, e], g.w2[e].rearrange("(f p) d -> p f d", p=P)).then_inc(g.w2_in.sem, 16)

                def step(it):
                    if not isinstance(it, int) or it < B:
                        dve_l["A"].wait(sp, it, ("add", TB - 1), ago=1)
                        settle(sp, payload_left)
                        sp.dma_start(x_sb, g.x.rearrange("(b t p) d -> p b t d", p=P, t=TB)
                                     [:, bass.ds(it, 1)].rearrange("p b t d -> p (b t) d")).then_inc(x_in, 16)
                    for h, ph, late in ((1, "B'", 2), (0, "B", 1)):
                        if not isinstance(it, int) or 0 <= it - late < B:
                            dve_l[ph].wait(sp, it, ("norm_2", h * G + G - 1), ago=late)
                            sp.dma_start(g.x2_dram.rearrange("(b h t p) d -> p (b h) t d", p=P, t=G, h=2)
                                         [:, bass.ds(it * 2 + (h - 2 * late), 1)].rearrange("p b t d -> p (b t) d"),
                                         x2[:, h * G:h * G + G, :]).then_inc(x2_out[h], 16)
                    if isinstance(it, int) and it == 0:
                        for e in range(NE - 1):
                            load_w2(e)

                def spare():
                    dve_l["A"].wait(sp, B - 1, ("add", TB - 1))
                    load_w2(NE - 1)
                    sp.wait_ge(pads_ready, 1)
                    at_row = NE * ROWS_E
                    sp.dma_start(g.xe_dram[at_row:at_row + SPARE * P, :].rearrange("(k p) d -> p k d", p=P),
                                 pad_rows[:, NE:NE + SPARE, :]).then_inc(spare_in, 16)
                over(sp, step, spare)
                sp.wait_ge(pads_at, 1)
                for e in range(NE):
                    row = sp.value_load(pad_i[0:1, e:e + 1], min_val=0, max_val=X_ROWS - P)
                    sp.dma_start(g.xe_dram[bass.ds(row, P), :], pad_rows[:, e, :]).then_inc(pads_in, 16)
                sp.wait_ge(pads_in, 16 * NE)
                for h in range(2):
                    sp.wait_ge(x2_out[h], 16 * B)
                sp.wait_ge(spare_in, 16)

            @block.tensor
            def _(pe):
                def turn(src, ph):
                    for k in range(KD):
                        mm = pe.transpose(pT[ph][:, k, :], src[:, k * P:(k + 1) * P], g.ident[:, :])
                    return mm

                def product(out, ph, rhs, last=None):
                    for k in range(KD):
                        mm = pe.matmul(out, turned[ph][:, k, :], rhs(k), start=k == 0, stop=last is None and k == KD - 1)
                    if last:
                        mm = pe.matmul(out, g.ones[0:1, :], last, start=False, stop=True)
                    return mm

                def turn_a(it, t):
                    act_l["A"].wait(pe, it, ("gather", t))
                    act_l["A"].wait(pe, it, **before("copy_a", t, 0))
                    return turn(at, "A")

                def proj(it, t):
                    act_l["A"].wait(pe, it, ("copy_a", t))
                    dve_l["A"].wait(pe, it, **before("add", t, 0))
                    return product(pO["A"][:, :], "A", lambda k: g.woT_sb[:, k, :])

                def turn_1(it, t):
                    ph, norm = half(t, "A", 1)
                    dve_l[ph].wait(pe, it, **norm)
                    act_l["B"].wait(pe, it, **before("copy_1", t, 1))
                    return turn(x1[:, t], "B")

                def score(it, t):
                    act_l["B"].wait(pe, it, ("copy_1", t), ago=1)
                    act_l["B"].wait(pe, it, **before("soft", t, 1))
                    own = bass.ds(it * C - C, C)
                    return product(pS[:, 0:C], "B", lambda k: g.fold[:, k, own], g.fold_b[:, own])

                def turn_p(it, t):
                    act_l["B"].wait(pe, it, ("soft", t), ago=1)
                    act_l["B"].wait(pe, it, **before("copy_p", t, 1))
                    return pe.transpose(pPT[:, :], pr[:, :], g.ident[:, :])

                def cross(it, t):
                    act_l["B"].wait(pe, it, ("copy_p", t), ago=1)
                    dve_l["B"].wait(pe, it, **before("mix", t, 1))
                    return pe.matmul(pO["B"][:, :], prT[:, :],
                                     g.cv[:, bass.ds(it - 1, 1), :].rearrange("c b d -> c (b d)"), start=True, stop=True)

                def turn_2(it, t):
                    ph, norm = half(t, "B", 2)
                    dve_l[ph].wait(pe, it, **norm)
                    act_l["C"].wait(pe, it, **before("copy_2", t, 2))
                    return turn(x2[:, t], "C")

                def gate(it, t):
                    act_l["C"].wait(pe, it, ("copy_2", t), ago=2)
                    if t == 0:
                        dve_l["C"].wait(pe, it, ("pos",), ago=3)
                    return product(pG[:, 0, t, :], "C", lambda k: g.gate_sb[:, k, :])

                def rank(it):
                    dve_l["C"].wait(pe, it, ("both",), ago=2)
                    return pe.matmul(pG[:, 1].rearrange("p t e -> p (t e)"), g.below[:, :],
                                     both[:, :, :].rearrange("p t e -> p (t e)"), start=True, stop=True)

                def total(it):
                    return pe.matmul(pG[:, 2].rearrange("p t e -> p (t e)"), g.ones[:, :],
                                     both[:, :, :].rearrange("p t e -> p (t e)"), start=True, stop=True)

                def keep_warm(it, n, ago):
                    if isinstance(it, int):
                        ago = max(ago, it - B + 1)
                    act_l["B"].wait(pe, it, ("soft", TB - 1), ago=ago)
                    for _ in range(n):
                        pe.matmul(pS[:, P:P + D], g.ident[:, :], g.woT_sb[:, 0, :], start=True, stop=True)

                ops = {"keep_warm": keep_warm, "turn_a": turn_a, "proj": proj, "turn_1": turn_1, "score": score, "turn_p": turn_p,
                       "cross": cross, "turn_2": turn_2, "gate": gate, "rank": rank, "total": total}
                start(pe_l)(pe)
                pe.wait_ge(set_up, 3)
                over(pe, lambda it: body(it, pe_l, pe_t, ops))

            @block.scalar
            def _(act):
                def gather(it, t):
                    pe_l["A"].wait(act, it, **before("turn_a", t, 0))
                    return act.copy(at[:, :].rearrange("p (h d) -> p h d", h=H), g.attn[:, bass.ds(it * H, H), t, :])

                def take(ph):
                    return act.copy(turned[ph][:, :, :], pT[ph][:, :, :])

                def copy_a(it, t):
                    pe_l["A"].wait(act, it, ("turn_a", t))
                    pe_l["A"].wait(act, it, **before("proj", t, 0))
                    return take("A")

                def copy_1(it, t):
                    pe_l["B"].wait(act, it, ("turn_1", t), ago=1)
                    pe_l["B"].wait(act, it, **before("score", t, 1))
                    return take("B")

                def copy_2(it, t):
                    pe_l["C"].wait(act, it, ("turn_2", t), ago=2)
                    pe_l["C"].wait(act, it, **before("gate", t, 2))
                    return take("C")

                def soft(it, t):
                    dve_l["B"].wait(act, it, ("max", t), ago=1)
                    pe_l["B"].wait(act, it, **before("turn_p", t, 1))
                    return act.activation(pr[:, 0:C], pS[:, 0:C], ACT.Exp,
                                          bias=cneg[:, t:t + 1], accum_out=csum[:, t:t + 1])

                def copy_p(it, t):
                    pe_l["B"].wait(act, it, ("turn_p", t), ago=1)
                    pe_l["B"].wait(act, it, **before("cross", t, 1))
                    return act.copy(prT[:, :], pPT[:, :])

                def fill_0(it, t):
                    ph, norm = half(t, "B", 2)
                    dve_l[ph].wait(act, it, **norm)
                    act.wait_ge(scattered[t], it * 32 - 64)
                    return act.copy(pay[0][:, t, 0:D], x2[:, t])

                def fill_1(it, t):
                    return act.copy(pay[1][:, t, 0:D], x2[:, t])

                def gap_exp(it):
                    dve_l["C"].wait(act, it, ("gap",), ago=2)
                    return act.activation(gap_e[:, :], gap[:, :], ACT.Exp)

                ops = {"gather": gather, "copy_a": copy_a, "copy_1": copy_1, "soft": soft, "copy_p": copy_p,
                       "copy_2": copy_2, "fill_0": fill_0, "fill_1": fill_1, "gap_exp": gap_exp}
                start(act_l)(act)
                over(act, lambda it: body(it, act_l, act_last if isinstance(it, int) and it == B + 1 else act_t, ops))

            @block.vector
            def _(dve):
                dve_a, dve_b, dve_c = (dve_l[ph] for ph in "ABC")

                def add(it, t):
                    pe_l["A"].wait(dve, it, ("proj", t))
                    if t == 0:
                        dve.wait_ge(x_in, it * 16 + 16)
                    dve_b.wait(dve, it, ("mix", t), ago=1)
                    return dve.tensor_tensor(x1[:, t], pO["A"][:, :], x_sb[:, t], ALU.add)

                def stat_1(it, t):
                    dve_a.wait(dve, it, ("add", t))
                    return dve.bn_stats(stats["A"][:, t, :], x1[:, t])

                def aggr(it, ph, t, ago):
                    if t == 0:
                        pool_l[ph].wait(dve, it, ("rstd", 1), ago=ago + 1)
                    settle(dve, g.settled)
                    return dve.bn_aggr(mv[ph][:, t, :], stats[ph][:, t, :])

                def aggr_1(it, t):
                    dve_a.wait(dve, it, ("stat_1", t))
                    return aggr(it, "A", t, 0)

                def normalise(it, ph, t, x, ago):
                    pool_l[ph].wait(dve, it, ("rstd", t // G), ago=ago)
                    return dve.tensor_scalar(x, x, mv[ph][:, t, 0:1], rstd[ph][:, t:t + 1], ALU.subtract, ALU.mult)

                def norm_1(it, t):
                    return normalise(it, "A", t, x1[:, t], 0 if t < G else 1)

                def max_(it, t):
                    pe_l["B"].wait(dve, it, ("score", t), ago=1)
                    return dve.tensor_reduce(cneg[:, t:t + 1], pS[:, 0:C], AX.X, ALU.max, negate=True)

                def rec(it, t):
                    act_l["B"].wait(dve, it, ("soft", t), ago=1)
                    return dve.reciprocal(crec[:, t:t + 1], csum[:, t:t + 1])

                def mix(it, t):
                    dve_b.wait(dve, it, ("rec", t), ago=1)
                    pe_l["B"].wait(dve, it, ("cross", t), ago=1)
                    if t % G == 0:
                        dve.wait_ge(x2_out[t // G], it * 16 - 16)
                    return dve.scalar_tensor_tensor(x2[:, t], pO["B"][:, :], crec[:, t:t + 1], x1[:, t],
                                                    ALU.mult, ALU.add)

                def stat_2(it, t):
                    dve_b.wait(dve, it, ("mix", t), ago=1)
                    return dve.bn_stats(stats["B"][:, t, :], x2[:, t])

                def aggr_2(it, t):
                    dve_b.wait(dve, it, ("stat_2", t), ago=1)
                    return aggr(it, "B", t, 1)

                def norm_2(it, t):
                    return normalise(it, "B", t, x2[:, t], 1 if t < G else 2)

                def row(it, i):
                    if i == 0:
                        act_l["F"].wait(dve, it, ("fill_1", TB - 1), ago=2)
                    first = g.col["token"].start - 2 * TB
                    return dve.tensor_scalar(pay[i][:, :, D].bitcast(I32), g.step_c[:, bass.ds(it * TB + first, TB)],
                                             float(i), None, ALU.add)

                def logits(it):
                    pe_l["C"].wait(dve, it, ("gate", TB - 1), ago=2)
                    return dve.tensor_tensor(lg[:, :, :], pG[:, 0], by_tile(g.gate_b_sb[:, :]), ALU.add)

                def top_(it, t):
                    if t == 0:
                        dve_c.wait(dve, it, ("logits",), ago=2)
                        settle(dve, g.settled)
                    return dve.max(top[:, t, :], lg[:, t, :])

                def top_i_(it, t):
                    dve_c.wait(dve, it, ("top", t), ago=2)
                    settle(dve, g.settled)
                    return dve.max_index(top_i[:, t, :], top[:, t, :], lg[:, t, :])

                def top_f_(it):
                    dve_c.wait(dve, it, ("top_i", TB - 1), ago=2)
                    return dve.tensor_copy(top_f[:, :, :], top_i[:, :, 0:2])

                def by_expert(ap):
                    return ap.rearrange("p (t o) -> p t o", o=1).to_broadcast([P, TB, NE])

                def by_tile(ap):
                    return ap.rearrange("p (o e) -> p o e", o=1).to_broadcast([P, TB, NE])

                def hot_(it, i):
                    dve_c.wait(dve, it, ("top_f",), ago=2)
                    return dve.tensor_tensor(hot[i][:, :, :], by_expert(top_f[:, :, i]), by_tile(g.step_c[:, g.col["iota8"]]),
                                             ALU.is_equal)

                def both_(it):
                    dve_c.wait(dve, it, ("hot_1",), ago=2)
                    return dve.tensor_tensor(both[:, :, :], hot[0][:, :, :], hot[1][:, :, :], ALU.add)

                def gap_(it):
                    act_l["C"].wait(dve, it, ("gap_exp",), ago=3)
                    return dve.tensor_tensor(gap[:, :], top[:, :, 1], top[:, :, 0], ALU.subtract)

                def count_0(it):
                    dve_c.wait(dve, it, ("run",), ago=3)
                    return dve.tensor_copy(count[:, :, 0], g.run[:, :])

                def count_(it):
                    pe_l["C"].wait(dve, it, ("total",), ago=2)
                    return dve.tensor_copy(count[:, :, 1:TB + 1], pG[:, 2].rearrange("p t e -> p e t"))

                def base_(it):
                    dve_c.wait(dve, it, ("count",), ago=2)
                    settle(dve, g.settled)
                    flat = "p e t -> p (e t)"
                    return dve.tensor_tensor_scan(base[:, :, :].rearrange(flat), g.step_c[:, g.col["anew"]],
                                                  count[:, :, :].rearrange(flat), 0.0, ALU.mult, ALU.add)

                def run_(it):
                    dve_c.wait(dve, it, ("base",), ago=2)
                    return dve.tensor_copy(g.run[:, :], base[:, :, TB])

                def pos_(it):
                    dve_c.wait(dve, it, ("base",), ago=2)
                    return dve.tensor_tensor(pos[:, :, :], pG[:, 1], base[:, :, 0:TB].rearrange("p e t -> p t e"), ALU.add)

                def region(it):
                    dve_c.wait(dve, it, ("pos",), ago=2)
                    return dve.tensor_tensor(pos[:, :, :], pos[:, :, :], by_tile(g.step_c[:, g.col["region"]]), ALU.add)

                def pick(it, i):
                    dve_c.wait(dve, it, ("sum_0",) if i else ("region",), ago=2)
                    return dve.tensor_tensor(picked[:, :, :], pos[:, :, :], hot[i][:, :, :], ALU.mult)

                def sum_(it, i):
                    dve_c.wait(dve, it, (f"pick_{i}",), ago=2)
                    return dve.tensor_reduce(pos_f[:, i, :], picked[:, :, :], AX.X, ALU.add)

                def pos_i_(it):
                    dve_c.wait(dve, it, ("sum_1",), ago=2)
                    return dve.tensor_copy(pos_i[:, :, :], pos_f[:, :, :])

                def weights(i, it):
                    return g.c_sum[:, i, bass.ds(it * TB - 2 * TB, TB)]

                def one_plus(it):
                    act_l["C"].wait(dve, it, ("gap_exp",), ago=2)
                    return dve.tensor_scalar(gap[:, :], gap_e[:, :], 1.0, None, ALU.add)

                def w_first(it):
                    dve_c.wait(dve, it, ("one_plus",), ago=2)
                    return dve.reciprocal(weights(0, it), gap[:, :])

                def w_second(it):
                    dve_c.wait(dve, it, ("w_first",), ago=2)
                    return dve.tensor_tensor(weights(1, it), gap_e[:, :], weights(0, it), ALU.mult)

                ops = {"add": add, "stat_1": stat_1, "aggr_1": aggr_1, "norm_1": norm_1, "max": max_, "rec": rec, "mix": mix, "stat_2": stat_2, "aggr_2": aggr_2, "norm_2": norm_2,
                       "logits": logits, "top": top_, "top_i": top_i_, "top_f": top_f_, "both": both_,
                       "gap": gap_, "count_0": count_0, "count": count_, "base": base_, "run": run_, "pos": pos_, "region": region,
                       "pos_i": pos_i_, "one_plus": one_plus, "w_first": w_first, "w_second": w_second}
                for i in range(2):
                    ops[f"hot_{i}"] = lambda it, i=i: hot_(it, i)
                    ops[f"pick_{i}"] = lambda it, i=i: pick(it, i)
                    ops[f"sum_{i}"] = lambda it, i=i: sum_(it, i)
                    ops[f"row_{i}"] = lambda it, i=i: row(it, i)

                def pad_ids():
                    act_l["A"].wait(dve, B - 1, ("gather", TB - 1))
                    dve.tensor_copy(pad_rows[:, :, D].bitcast(I32), g.step_c[:, g.col["pads"]]).then_inc(pads_ready, 1)

                start(dve_l)(dve)
                dve.memset(eps[:, :], EPS).then_inc(set_up, 1)
                dve.memset(pay[1][:, :, D:PAYLOAD], 0.0).then_inc(set_up, 1)
                dve.memset(pr[:, C:CP], 0.0).then_inc(set_up, 1)
                dve.wait_ge(set_up, 3)
                over(dve, lambda it: body(it, dve_l, dve_t, ops), pad_ids)
                dve_c.wait(dve, B + 1, ("w_second",), ago=2)
                tile_table(nc, dve, g, st, pad_i, x1, pads_at)

            @block.gpsimd
            def _(pool):
                def var(it, ph, h):
                    dve_l[ph].wait(pool, it, (f"aggr_{1 + LAG[ph]}", h * G + G - 1), ago=LAG[ph])
                    return pool.tensor_tensor(dev[ph][:, h * G:h * G + G], mv[ph][:, h * G:h * G + G, 1], eps[:, 0:G], ALU.add)

                def rstd_(it, ph, h):
                    pool_l[ph].wait(pool, it, ("var", h), ago=LAG[ph])
                    return pool.tensor_tensor(rstd[ph][:, h * G:h * G + G], dev[ph][:, h * G:h * G + G], g.neg_half[:, 0:G], ALU.pow)

                def step(it):
                    for ph, (kind, h) in pool_t:
                        if not isinstance(it, int) or 0 <= it - LAG[ph] < B:
                            (var if kind == "var" else rstd_)(it, ph, h).then_inc(pool_l[ph].sem, 1)
                    if not isinstance(it, int) or it >= 2:
                        dve_l["C"].wait(pool, it, ("pos_i",), ago=2)
                        act_l["F"].wait(pool, it, ("fill_1", TB - 1), ago=2)
                        settle(pool, payload_left)
                        for t in T:
                            for i in range(2):
                                pool.indirect_dma_start(g.xe_dram, bass.IndirectOffsetOnAxis(pos_i[:, i, t:t + 1], 0),
                                                        pay[i][:, t, :], None, bounds_check=X_ROWS - 1
                                                        ).then_inc(scattered[t], 16)

                start(pool_l)(pool)
                pool.wait_ge(set_up, 2)
                over(pool, step)
                for t in T:
                    pool.wait_ge(scattered[t], 32 * B)


def tile_table(nc, dve, g, st, pad_i, room, pads_at):
    def sb(n, s, d=F32): return st.enter_context(nc.sbuf_tensor(n, s, d))
    step = Ticks(st.enter_context(nc.semaphore("table_ops")))
    T = FFN_TILES
    full = sb("full", [P, NE])
    full_i = sb("full_i", [P, NE], I32)
    tiles = sb("tiles_e", [P, NE])
    cum = sb("cum", [P, NE])
    past = room[:, :, :].rearrange("p t d -> p (t d)")[:, 0:T * NE].rearrange("p (t e) -> p t e", e=NE)
    expert = sb("expert", [P, T])
    before = sb("before", [P, T])
    row = sb("row", [P, T])
    n = 0

    def then(ins):
        nonlocal n
        n += 1
        ins.then_inc(step.sem, 1)
        step.wait(dve, 0, n)

    def wide(ap, left):
        return (ap.rearrange("p (t o) -> p t o", o=1) if left else ap.rearrange("p (o e) -> p o e", o=1)).to_broadcast([P, T, NE])

    then(dve.tensor_tensor(full[:, :], g.run[:, :], g.step_c[:, g.col["region"]], ALU.add))
    dve.tensor_copy(pad_i[:, :], full[:, :]).then_inc(pads_at, 1)
    then(dve.tensor_scalar(full_i[:, :], g.run[:, :], float(P - 1), None, ALU.add))
    then(dve.tensor_single_scalar(full_i[:, :], full_i[:, :], P.bit_length() - 1, ALU.arith_shift_right))
    then(dve.tensor_copy(tiles[:, :], full_i[:, :]))
    then(dve.tensor_tensor_scan(cum[:, :], g.ones[:, 0:NE], tiles[:, :], 0.0, ALU.mult, ALU.add))
    then(dve.tensor_tensor(past, wide(g.step_c[:, g.col["tiles"]], True), wide(cum[:, :], False), ALU.is_ge))
    then(dve.tensor_reduce(expert[:, :], past, AX.X, ALU.add))
    then(dve.tensor_tensor(past, past, wide(tiles[:, :], False), ALU.mult))
    then(dve.tensor_reduce(before[:, :], past, AX.X, ALU.add))
    then(dve.tensor_tensor(row[:, :], g.step_c[:, g.col["tiles"]], before[:, :], ALU.subtract))
    then(dve.tensor_scalar(row[:, :], row[:, :], float(P), None, ALU.mult))
    then(dve.scalar_tensor_tensor(g.table[:, 0, :], expert[:, :], float(ROWS_E), row[:, :], ALU.mult, ALU.add))
    then(dve.tensor_scalar(g.table[:, 1, :], expert[:, :], float(NE - 1), None, ALU.min))


def experts(nc, g):
    U = 8
    IT = -(-FFN_TILES // U)
    XS = 4
    with ExitStack() as st:
        def sb(n, s, d=F32): return st.enter_context(nc.sbuf_tensor(n, s, d))
        def ps(n, s, d=F32): return st.enter_context(nc.psum_tensor(n, s, d))
        def sem(n, **kw): return Ticks(st.enter_context(nc.semaphore(n)), **kw)

        b2_sb = sb("b2_sb", [P, NE, D])
        xg = [sb(f"xg{i}", [P, PAYLOAD]) for i in range(XS)]
        y_row = [sb(f"y_row{i}", [P, 1], I32) for i in range(XS)]
        xgT = [sb(f"xgT{i}", [P, KD, P]) for i in range(2)]
        w1_e = [g.attn[:, (2 + i) * H:(3 + i) * H].rearrange("p h t d -> p (h t d)").rearrange("p (k f) -> p k f", k=KD)
                for i in range(2)]
        hT = [sb(f"hT{i}", [P, FT, P]) for i in range(2)]
        y = [sb(f"y{i}", [P, D]) for i in range(2)]
        pX = [ps(f"pX{i}", [P, KD, P]) for i in range(2)]
        pH = [ps(f"pH{i}", [P, FT, P]) for i in range(2)]
        pY = [ps(f"pY{i}", [P, D]) for i in range(2)]

        turned, up_done, down_done = sem("ex_turned", per=U), sem("ex_up", per=U), sem("ex_down", per=U)
        x_taken, relu_done = sem("ex_x_taken", per=U), sem("ex_relu", per=U)
        w1_copied, kept, result_done = sem("ex_w1", per=U), sem("ex_kept", per=U), sem("ex_result", per=U)
        x_in = [sem(f"xg_in{i}", per=U // XS, by=16) for i in range(XS)]
        out = [sem(f"y_out{i}", per=U // XS, by=16) for i in range(XS)]
        b2_in = sem("b2_in")
        settled_pool, settled_sp = sem("settled_pool"), sem("settled_sp")

        def exists(it, tile):
            return not isinstance(it, int) or 0 <= it * U + tile < FFN_TILES

        def over(eng, body):
            body(0)
            with eng.Fori(1, IT - 1) as it:
                body(it)
            body(IT - 1)

        def slot(ticks, eng, it, tile):
            ticks[tile % XS].wait(eng, it, tile // XS + 1)

        def number(eng, it, tile, which):
            top = X_ROWS - P if which == 0 else NE - 1
            return eng.value_load(g.table[0:1, which, bass.ds(it * U + tile, 1)], min_val=0, max_val=top)

        with nc.Block() as block:
            @block.sync
            def _(sp):
                sp.dma_start(b2_sb[:, :, :].rearrange("p e d -> p (e d)"),
                             g.b2.rearrange("(a e) d -> a (e d)", a=1).to_broadcast([P, NE * D])).then_inc(b2_in.sem, 16)

                def load(it, tile):
                    row = number(sp, it, tile, 0)
                    if exists(it, tile - XS):
                        kept.wait(sp, it, tile - XS + 1)
                        settle(sp, settled_sp.sem)
                        turned.wait(sp, it, tile - XS + 1)
                        settle(sp, settled_sp.sem)
                    sp.dma_start(xg[tile % XS][:, :], g.xe_dram[bass.ds(row, P), :]).then_inc(x_in[tile % XS].sem, 16)

                for t in range(3):
                    load(0, t)
                half = NT // 2
                sp.dma_start(g.x2_tiles[:, 0:half, :], g.x2_dram[0:half * P, :].rearrange("(t p) d -> p t d", p=P)
                             ).then_inc(g.x2_in.sem, 16)

                def body(it):
                    for u in range(U):
                        if exists(it, u + 3):
                            load(it, u + 3)
                over(sp, body)

            @block.tensor
            def _(pe):
                def turn_x(it, tile):
                    slot(x_in, pe, it, tile)
                    x_taken.wait(pe, it, tile - 1)
                    for k in range(KD):
                        mm = pe.transpose(pX[tile % 2][:, k, :], xg[tile % XS][:, k * P:(k + 1) * P], g.ident[:, :])
                    mm.then_inc(turned.sem, 1)

                def up(it, tile):
                    x_taken.wait(pe, it, tile + 1)
                    w1_copied.wait(pe, it, tile + 1)
                    relu_done.wait(pe, it, tile - 1)
                    for f in range(FT):
                        for k in range(KD):
                            mm = pe.matmul(pH[tile % 2][:, f, :], w1_e[tile % 2][:, k, f * P:(f + 1) * P],
                                           xgT[tile % 2][:, k, :], start=k == 0, stop=k == KD - 1)
                    mm.then_inc(up_done.sem, 1)

                def down(it, tile):
                    e = number(pe, it, tile, 1)
                    relu_done.wait(pe, it, tile + 1)
                    result_done.wait(pe, it, tile - 1)
                    for f in range(FT):
                        mm = pe.matmul(pY[tile % 2][:, :], hT[tile % 2][:, f, :],
                                       g.w2_sb[:, bass.ds(e, 1), f, :].rearrange("p e d -> p (e d)"),
                                       start=f == 0, stop=f == FT - 1)
                    mm.then_inc(down_done.sem, 1)

                g.w2_in.wait(pe, 0, NE)
                turn_x(0, 0)
                turn_x(0, 1)
                up(0, 0)

                def body(it):
                    for u in range(U):
                        if exists(it, u + 1):
                            up(it, u + 1)
                        if exists(it, u + 2):
                            turn_x(it, u + 2)
                        if exists(it, u):
                            down(it, u)
                over(pe, body)

            @block.scalar
            def _(act):
                def copy_x(it, tile):
                    turned.wait(act, it, tile + 1)
                    up_done.wait(act, it, tile - 1)
                    act.copy(xgT[tile % 2][:, :, :], pX[tile % 2][:, :, :]).then_inc(x_taken.sem, 1)

                def relu(it, tile):
                    e = number(act, it, tile, 1)
                    up_done.wait(act, it, tile + 1)
                    down_done.wait(act, it, tile - 1)
                    for f in range(FT):
                        ins = act.activation(hT[tile % 2][:, f, :], pH[tile % 2][:, f, :], ACT.Relu,
                                             bias=g.b1_sb[:, bass.ds(e * FT + f, 1)])
                    ins.then_inc(relu_done.sem, 1)

                copy_x(0, 0)
                copy_x(0, 1)
                relu(0, 0)

                def body(it):
                    for u in range(U):
                        if exists(it, u + 2):
                            copy_x(it, u + 2)
                        if exists(it, u + 1):
                            relu(it, u + 1)
                over(act, body)

            @block.vector
            def _(dve):
                def copy_w1(it, tile):
                    e = number(dve, it, tile, 1)
                    up_done.wait(dve, it, tile - 1)
                    dve.tensor_copy(w1_e[tile % 2][:, :, :], g.w1_sb[:, bass.ds(e, 1)].rearrange("p e k f -> p (e k) f")
                                    ).then_inc(w1_copied.sem, 1)

                def keep(it, tile):
                    slot(x_in, dve, it, tile)
                    if exists(it, tile - XS):
                        slot(out, dve, it, tile - XS)
                    dve.tensor_copy(y_row[tile % XS][:, :], xg[tile % XS][:, D:D + 1].bitcast(I32)).then_inc(kept.sem, 1)

                def result(it, tile):
                    e = number(dve, it, tile, 1)
                    down_done.wait(dve, it, tile + 1)
                    if exists(it, tile - 2):
                        slot(out, dve, it, tile - 2)
                    dve.tensor_tensor(y[tile % 2][:, :], pY[tile % 2][:, :],
                                      b2_sb[:, bass.ds(e, 1), :].rearrange("p e d -> p (e d)"), ALU.add
                                      ).then_inc(result_done.sem, 1)

                g.w1_in.wait(dve, 0, g.w1_loads)
                copy_w1(0, 0)
                copy_w1(0, 1)
                dve.wait_ge(b2_in.sem, 16)
                keep(0, 0)
                keep(0, 1)

                def body(it):
                    for u in range(U):
                        if exists(it, u + 2):
                            copy_w1(it, u + 2)
                            keep(it, u + 2)
                        if exists(it, u):
                            result(it, u)
                over(dve, body)

            @block.gpsimd
            def _(pool):
                def scatter(it, tile):
                    result_done.wait(pool, it, tile + 1)
                    settle(pool, settled_pool.sem)
                    pool.indirect_dma_start(g.ye_dram, bass.IndirectOffsetOnAxis(y_row[tile % XS][:, :], 0),
                                            y[tile % 2][:, :], None, bounds_check=Y_ROWS - 1).then_inc(out[tile % XS].sem, 16)

                def body(it):
                    for u in range(U):
                        if exists(it, u):
                            scatter(it, u)
                over(pool, body)
                for tile in range(FFN_TILES - XS, FFN_TILES):
                    slot(out, pool, 0, tile)


def combine(nc, g):
    GT, U = 4, 4
    IT = NT // GT // U
    with ExitStack() as st:
        def sb(n, s, d=F32): return st.enter_context(nc.sbuf_tensor(n, s, d))
        def sem(n): return st.enter_context(nc.semaphore(n))

        xr = g.x2_tiles
        yr = sb("yr", [P, NT, 2, D])
        stats = [sb(f"c_stats{i}", [P, GT, 6]) for i in range(U)]
        mv = [sb(f"c_mv{i}", [P, GT, 2]) for i in range(U)]
        dev = [sb(f"c_dev{i}", [P, GT]) for i in range(U)]
        neg_mean = [sb(f"c_neg_mean{i}", [P, GT]) for i in range(U)]
        rstd = [sb(f"c_rstd{i}", [P, GT]) for i in range(U)]
        shift = [sb(f"c_shift{i}", [P, GT]) for i in range(U)]
        eps = sb("c_eps", [P, GT])
        minus = sb("c_minus", [P, GT])

        R, T = range(U), range(GT)
        dve_l = Line(sem("cb_dve"), [x for u in R for x in
                     [("sum", i, u, t) for i in range(2) for t in T] + [("stat", u, t) for t in T]
                     + [("aggr", u, t) for t in T]])
        pool_l = Line(sem("cb_pool"), [(k, u) for u in R for k in ("var", "neg_mean", "rstd", "shift")])
        act_l = Line(sem("cb_act"), [("norm", u, t) for u in R for t in T])
        loaded = [Ticks(sem(f"cb_in{u}"), per=1, by=32) for u in R]
        stored = [Ticks(sem(f"cb_out{u}"), per=1, by=16) for u in R]
        set_up, settled_sp, settled_act = sem("cb_set_up"), sem("cb_settled_sp"), sem("cb_settled_act")

        def rows(dram, it, u):
            return dram.rearrange("(g t p) d -> p g t d", p=P, t=GT)[:, bass.ds(it * U + u, 1)].rearrange("p g t d -> p (g t) d")

        def group(buf, it, u):
            return buf[:, bass.ds((it * U + u) * GT, GT)]

        with nc.Block() as block:
            @block.sync
            def _(sp):
                y_rows = g.ye_dram[0:2 * B * S, :].rearrange("(n two) d -> n (two d)", two=2)

                def load_y(it, u):
                    sp.dma_start(group(yr, it, u).rearrange("p t s d -> p t (s d)"), rows(y_rows, it, u)
                                 ).then_inc(loaded[u].sem, 16)

                for u in R:
                    load_y(0, u)
                    sp.sem_inc(loaded[u].sem, 16)
                with sp.Fori(1, IT) as it:
                    for u in R:
                        loaded[u].wait(sp, it, 0)
                        settle(sp, settled_sp)
                        sp.dma_start(group(xr, it, u), rows(g.x2_dram, it, u)).then_inc(loaded[u].sem, 16)
                        load_y(it, u)

            @block.vector
            def _(dve):
                def sum_(it, i, u, t):
                    if i == 0 and t == 0:
                        loaded[u].wait(dve, it, 1)
                    if i:
                        dve_l.wait(dve, it, ("sum", 0, u, t))
                    tile = (it * U + u) * GT + t
                    x = xr[:, bass.ds(tile, 1)].rearrange("p t d -> p (t d)")
                    return dve.scalar_tensor_tensor(x, yr[:, bass.ds(tile, 1), i].rearrange("p t d -> p (t d)"),
                                                    g.c_sum[:, i, bass.ds(tile, 1)], x, ALU.mult, ALU.add)

                def stat(it, u, t):
                    dve_l.wait(dve, it, ("sum", 1, u, t))
                    settle(dve, g.settled)
                    return dve.bn_stats(stats[u][:, t, :], xr[:, bass.ds((it * U + u) * GT + t, 1)].rearrange("p t d -> p (t d)"))

                def aggr(it, u, t):
                    dve_l.wait(dve, it, ("stat", u, t))
                    if t == 0:
                        act_l.wait(dve, it, ("norm", u, GT - 1), ago=1)
                        pool_l.wait(dve, it, ("shift", u), ago=1)
                    settle(dve, g.settled)
                    return dve.bn_aggr(mv[u][:, t, :], stats[u][:, t, :])

                dve_l.begin(dve)
                dve.memset(eps[:, :], EPS).then_inc(set_up, 1)
                dve.memset(minus[:, :], -1.0).then_inc(set_up, 1)
                dve.wait_ge(g.x2_in.sem, 16)
                with dve.Fori(0, IT) as it:
                    dve_l.emit(it, {"sum": sum_, "stat": stat, "aggr": aggr})

            @block.gpsimd
            def _(pool):
                def var(it, u):
                    dve_l.wait(pool, it, ("aggr", u, GT - 1))
                    return pool.tensor_tensor(dev[u][:, :], mv[u][:, :, 1], eps[:, :], ALU.add)

                def neg_mean_(it, u):
                    return pool.tensor_tensor(neg_mean[u][:, :], mv[u][:, :, 0], minus[:, :], ALU.mult)

                def rstd_(it, u):
                    pool_l.wait(pool, it, ("var", u))
                    act_l.wait(pool, it, ("norm", u, GT - 1), ago=1)
                    return pool.tensor_tensor(rstd[u][:, :], dev[u][:, :], g.neg_half[:, 0:GT], ALU.pow)

                def shift_(it, u):
                    pool_l.wait(pool, it, ("rstd", u))
                    return pool.tensor_tensor(shift[u][:, :], neg_mean[u][:, :], rstd[u][:, :], ALU.mult)

                pool_l.begin(pool)
                pool.wait_ge(set_up, 2)
                with pool.Fori(0, IT) as it:
                    pool_l.emit(it, {"var": var, "neg_mean": neg_mean_, "rstd": rstd_, "shift": shift_})

            @block.scalar
            def _(act):
                def norm(it, u, t):
                    if t == 0:
                        pool_l.wait(act, it, ("shift", u))
                    x = xr[:, bass.ds((it * U + u) * GT + t, 1)].rearrange("p t d -> p (t d)")
                    return act.activation(x, x, ACT.Identity, scale=rstd[u][:, t:t + 1], bias=shift[u][:, t:t + 1])

                act_l.begin(act)
                with act.Fori(0, IT) as it:
                    for u in R:
                        for t in T:
                            norm(it, u, t).then_inc(act_l.sem, 1)
                        act_l.wait(act, it, ("norm", u, GT - 1))
                        settle(act, settled_act)
                        act.dma_start(rows(g.out, it, u), group(xr, it, u)).then_inc(stored[u].sem, 16)
                for s in stored:
                    s.wait(act, IT - 1, 1)


def kernel(**inputs):
    import concourse.bacc as bacc
    from concourse.bass_utils import run_bass_kernel_spmd

    a = {k: np.asarray(v) for k, v in inputs.items()}
    lay = np.ascontiguousarray
    f32 = np.float32
    p = np.arange(P)[:, None]
    steps = np.concatenate([
        np.broadcast_to(np.arange(NE), (P, NE)),
        np.broadcast_to(np.arange(NE) * ROWS_E, (P, NE)),
        np.broadcast_to(np.arange(FFN_TILES), (P, FFN_TILES)),
        2 * (p + P * np.arange(NT)),
        2 * B * S + p + P * np.arange(NE + SPARE),
        np.broadcast_to(np.arange(NE * (TB + 1)) % (TB + 1) > 0, (P, NE * (TB + 1)))], axis=1).astype(f32)
    arrays = {
        "x": lay(a["x"].reshape(B * S, D)),
        "xT": lay(a["x"].reshape(B * S, D).T),
        "wqT": lay(a["L0_attn_w_q"].T), "wkT": lay(a["L0_attn_w_k"].T),
        "wvT": lay(a["L0_attn_w_v"].T), "woT": lay(a["L0_attn_w_o"].T),
        "ctxT": lay(a["ctx_1024"].reshape(B * C, D).T),
        "cWqT": lay(a["L0_xattn_Wq"].T), "cbq": lay(a["L0_xattn_bq"].reshape(KD, P).T),
        "cWk": lay(a["L0_xattn_Wk"]), "cbk": lay(a["L0_xattn_bk"].reshape(KD, P).T),
        "cWv": lay(a["L0_xattn_Wv"]), "cbv": lay(a["L0_xattn_bv"]),
        "gate_w": lay(a["L0_ffn_gate_w"]), "gate_b": lay(a["L0_ffn_gate_b"]),
        "w1": lay(a["L0_ffn_w1"]),
        "b1T": lay(a["L0_ffn_b1"].reshape(NE, FT, P).transpose(2, 0, 1).reshape(P, NE * FT)),
        "w2": lay(a["L0_ffn_w2"]), "b2": lay(a["L0_ffn_b2"]),
        "eye": np.eye(P, dtype=f32), "lower": np.triu(np.ones((P, P), f32), 1), "steps": steps,
    }
    nc = bacc.Bacc("TRN2", target_bir_lowering=False, num_devices=1)
    given = {n: nc.dram_tensor(n, v.shape, mybir.dt.from_np(v.dtype), kind="ExternalInput").ap()
             for n, v in arrays.items()}
    out = nc.dram_tensor("out", (B * S, D), F32, kind="ExternalOutput").ap()
    build_program(nc, **given, out=out)
    result = run_bass_kernel_spmd(nc, [arrays], core_ids=[0])
    return result.results[0]["out"].reshape(B, S, D)
```
